# Optimizing a Trainium2 kernel written in Bass

```python
import numpy as np
import jax
import jax.numpy as jnp

def _softmax(x, axis=-1):
    return jax.nn.softmax(x, axis=axis)

def _gelu(x):
    return jax.nn.gelu(x, approximate=True)

def _silu(x):
    return jax.nn.silu(x)

def _sigmoid(x):
    return jax.nn.sigmoid(x)

def _layernorm(x, axis=-1, eps=1e-05):
    m = jnp.mean(x, axis=axis, keepdims=True)
    v = jnp.var(x, axis=axis, keepdims=True)
    return (x - m) / jnp.sqrt(v + eps)

def _scatter_add(tgt, idx, src, axis=0):
    return tgt.at[idx].add(src)

def _segment_sum(src, seg, n):
    return jax.ops.segment_sum(src, seg, n)
kernel_name = 'mk_prb_d2_jaxref_r8_b4dc7a'

def setup_inputs(seed: int=0):
    np.random.seed(seed)
    _w = jnp.asarray

    def _L0_attn_setup():
        import jax, jax.numpy as jnp
        import numpy as np
        import math
        B, L, D_MODEL = (2, 256, 128)
        NUM_HEADS = 16
        FEATURE_DIM = 16
        HEAD_DIM = D_MODEL // NUM_HEADS
        EPS = 1e-12

        def taylor_exp(x):
            d = x.shape[-1]
            r2 = math.sqrt(2.0)
            rd = math.sqrt(d)
            rrd = math.sqrt(rd)
            x2 = (x[..., :, None] * x[..., None, :]).reshape(*x.shape[:-1], d * d) / r2
            ones = jnp.ones_like(x[..., :1])
            return jnp.concatenate([ones, x / rrd, x2 / rd], axis=-1)
        key = jax.random.key(seed)
        k0, k1, k2, k3, k4 = jax.random.split(key, 5)
        hidden_states = jax.random.normal(k0, (B, L, D_MODEL), dtype=jnp.float32)
        s = 1.0 / math.sqrt(D_MODEL)
        Wq = jax.random.normal(k1, (FEATURE_DIM * NUM_HEADS, D_MODEL), dtype=jnp.float32) * s
        Wk = jax.random.normal(k2, (FEATURE_DIM * NUM_HEADS, D_MODEL), dtype=jnp.float32) * s
        Wv = jax.random.normal(k3, (NUM_HEADS * HEAD_DIM, D_MODEL), dtype=jnp.float32) * s
        Wo = jax.random.normal(k4, (D_MODEL, NUM_HEADS * HEAD_DIM), dtype=jnp.float32) * s
        return {'hidden_states': hidden_states, 'Wq': Wq, 'Wk': Wk, 'Wv': Wv, 'Wo': Wo}
    _L0_attn_in = _L0_attn_setup()

    def _L0_ffn_setup():
        import jax, jax.numpy as jnp
        import numpy as np
        TOP_K = 2
        N_GROUP = 4
        TOPK_GROUP = 2
        ROUTED_SCALE = 2.5

        def _gate(xf, gate_w, gate_bias):
            logits = xf.astype(jnp.float32) @ gate_w.astype(jnp.float32)
            scores = jax.nn.sigmoid(logits)
            sfc = scores + gate_bias.astype(jnp.float32)[None]
            T, E = sfc.shape
            e_g = E // N_GROUP
            group_feat = sfc.reshape(T, N_GROUP, e_g)
            group_scores = jax.lax.top_k(group_feat, 2)[0].sum(axis=-1)
            _, group_idx = jax.lax.top_k(group_scores, TOPK_GROUP)
            group_mask = jax.nn.one_hot(group_idx, N_GROUP, dtype=sfc.dtype).sum(axis=1)
            score_mask = jnp.broadcast_to(group_mask[..., None], (T, N_GROUP, e_g)).reshape(T, E)
            tmp_scores = jnp.where(score_mask > 0, sfc, 0.0)
            _, topk_idx = jax.lax.top_k(tmp_scores, TOP_K)
            topk_w = jnp.take_along_axis(sfc, topk_idx, axis=-1)
            topk_w = topk_w / (topk_w.sum(axis=-1, keepdims=True) + 1e-20)
            return (topk_idx, topk_w * ROUTED_SCALE)
        key = jax.random.key(seed)
        ks = jax.random.split(key, 9)
        B, N, H, I, E, SH_I = (2, 128, 128, 64, 8, 128)
        s = lambda k, shape, scale: jax.random.normal(k, shape, jnp.float32) * scale
        return {'x': s(ks[0], (B, N, H), 1.0), 'gate_w': s(ks[1], (H, E), 0.02), 'gate_bias': s(ks[2], (E,), 0.02), 'w_gate': s(ks[3], (E, H, I), 0.02), 'w_up': s(ks[4], (E, H, I), 0.02), 'w_down': s(ks[5], (E, I, H), 0.02), 'sw_gate': s(ks[6], (H, SH_I), 0.02), 'sw_up': s(ks[7], (H, SH_I), 0.02), 'sw_down': s(ks[8], (SH_I, H), 0.02)}
    _L0_ffn_in = _L0_ffn_setup()

    def _L1_attn_setup():
        import jax, jax.numpy as jnp
        import numpy as np
        HEADS = 16
        key = jax.random.key(seed)
        k1, k2, k3, k4 = jax.random.split(key, 4)
        C, T, E = (8, 512, 128)
        D = E // HEADS
        x = jax.random.normal(k1, (C, T, E), dtype=jnp.float32)
        Wq = jax.random.normal(k2, (D, D), dtype=jnp.float32) * (1.0 / np.sqrt(D))
        Wk = jax.random.normal(k3, (D, D), dtype=jnp.float32) * (1.0 / np.sqrt(D))
        Wv = jax.random.normal(k4, (D, D), dtype=jnp.float32) * (1.0 / np.sqrt(D))
        return {'x': x, 'Wq': Wq, 'Wk': Wk, 'Wv': Wv}
    _L1_attn_in = _L1_attn_setup()

    def _L1_ffn_setup():
        import jax, jax.numpy as jnp
        import numpy as np
        E, D, F, GATE_DIM = (8, 128, 512, 16)
        B, T = (2, 256)
        key = jax.random.key(seed)
        ks = jax.random.split(key, 7)
        s = 0.02
        return {'hidden_states': jax.random.normal(ks[0], (B, T, D), dtype=jnp.float32), 'w_red': jax.random.normal(ks[1], (D, GATE_DIM), dtype=jnp.float32) * s, 'wg': jax.random.normal(ks[2], (E, GATE_DIM), dtype=jnp.float32), 'w1': jax.random.normal(ks[3], (E, D, F), dtype=jnp.float32) * s, 'b1': jax.random.normal(ks[4], (E, F), dtype=jnp.float32) * s, 'w2': jax.random.normal(ks[5], (E, F, D), dtype=jnp.float32) * s, 'b2': jax.random.normal(ks[6], (E, D), dtype=jnp.float32) * s}
    _L1_ffn_in = _L1_ffn_setup()
    _d = {'L0_attn_hidden_states': _L0_attn_in['hidden_states'], 'L0_attn_Wq': _L0_attn_in['Wq'], 'L0_attn_Wk': _L0_attn_in['Wk'], 'L0_attn_Wv': _L0_attn_in['Wv'], 'L0_attn_Wo': _L0_attn_in['Wo'], 'L0_ffn_gate_w': _L0_ffn_in['gate_w'], 'L0_ffn_gate_bias': _L0_ffn_in['gate_bias'], 'L0_ffn_w_gate': _L0_ffn_in['w_gate'], 'L0_ffn_w_up': _L0_ffn_in['w_up'], 'L0_ffn_w_down': _L0_ffn_in['w_down'], 'L0_ffn_sw_gate': _L0_ffn_in['sw_gate'], 'L0_ffn_sw_up': _L0_ffn_in['sw_up'], 'L0_ffn_sw_down': _L0_ffn_in['sw_down'], 'L1_attn_Wq': _L1_attn_in['Wq'], 'L1_attn_Wk': _L1_attn_in['Wk'], 'L1_attn_Wv': _L1_attn_in['Wv'], 'L1_ffn_w_red': _L1_ffn_in['w_red'], 'L1_ffn_wg': _L1_ffn_in['wg'], 'L1_ffn_w1': _L1_ffn_in['w1'], 'L1_ffn_b1': _L1_ffn_in['b1'], 'L1_ffn_w2': _L1_ffn_in['w2'], 'L1_ffn_b2': _L1_ffn_in['b2']}
    _x0 = _d['L0_attn_hidden_states']
    _d['L0_attn_hidden_states'] = jax.random.normal(jax.random.fold_in(jax.random.key(seed), 1), (4, 512, 128), dtype=_x0.dtype)
    del _x0
    return _d

def reference(L0_attn_hidden_states, L0_attn_Wq, L0_attn_Wk, L0_attn_Wv, L0_attn_Wo, L0_ffn_gate_w, L0_ffn_gate_bias, L0_ffn_w_gate, L0_ffn_w_up, L0_ffn_w_down, L0_ffn_sw_gate, L0_ffn_sw_up, L0_ffn_sw_down, L1_attn_Wq, L1_attn_Wk, L1_attn_Wv, L1_ffn_w_red, L1_ffn_wg, L1_ffn_w1, L1_ffn_b1, L1_ffn_w2, L1_ffn_b2):

    def _L0_attn_ref(hidden_states, Wq, Wk, Wv, Wo):
        import jax, jax.numpy as jnp
        import numpy as np
        import math
        B, L, D_MODEL = (2, 256, 128)
        NUM_HEADS = 16
        FEATURE_DIM = 16
        HEAD_DIM = D_MODEL // NUM_HEADS
        EPS = 1e-12

        def taylor_exp(x):
            d = x.shape[-1]
            r2 = math.sqrt(2.0)
            rd = math.sqrt(d)
            rrd = math.sqrt(rd)
            x2 = (x[..., :, None] * x[..., None, :]).reshape(*x.shape[:-1], d * d) / r2
            ones = jnp.ones_like(x[..., :1])
            return jnp.concatenate([ones, x / rrd, x2 / rd], axis=-1)
        b, l, _ = hidden_states.shape
        q = (hidden_states @ Wq.T).reshape(b, l, NUM_HEADS, FEATURE_DIM).transpose(0, 2, 1, 3)
        k = (hidden_states @ Wk.T).reshape(b, l, NUM_HEADS, FEATURE_DIM).transpose(0, 2, 1, 3)
        v = (hidden_states @ Wv.T).reshape(b, l, NUM_HEADS, HEAD_DIM).transpose(0, 2, 1, 3)
        qf = taylor_exp(q)
        kf = taylor_exp(k)
        A = jnp.einsum('bhnd,bhmd->bhnm', qf, kf)
        A = jnp.tril(A)
        y = jnp.einsum('bhnm,bhme->bhne', A, v)
        z = 1.0 / (jnp.einsum('bhld,bhld->bhl', qf, jnp.cumsum(kf, axis=2)) + EPS)
        y = y * z[..., None]
        y = y.transpose(0, 2, 1, 3).reshape(b, l, NUM_HEADS * HEAD_DIM)
        return y @ Wo.T

    def _L0_ffn_ref(x, gate_w, gate_bias, w_gate, w_up, w_down, sw_gate, sw_up, sw_down):
        import jax, jax.numpy as jnp
        import numpy as np
        TOP_K = 2
        N_GROUP = 4
        TOPK_GROUP = 2
        ROUTED_SCALE = 2.5

        def _gate(xf, gate_w, gate_bias):
            logits = xf.astype(jnp.float32) @ gate_w.astype(jnp.float32)
            scores = jax.nn.sigmoid(logits)
            sfc = scores + gate_bias.astype(jnp.float32)[None]
            T, E = sfc.shape
            e_g = E // N_GROUP
            group_feat = sfc.reshape(T, N_GROUP, e_g)
            group_scores = jax.lax.top_k(group_feat, 2)[0].sum(axis=-1)
            _, group_idx = jax.lax.top_k(group_scores, TOPK_GROUP)
            group_mask = jax.nn.one_hot(group_idx, N_GROUP, dtype=sfc.dtype).sum(axis=1)
            score_mask = jnp.broadcast_to(group_mask[..., None], (T, N_GROUP, e_g)).reshape(T, E)
            tmp_scores = jnp.where(score_mask > 0, sfc, 0.0)
            _, topk_idx = jax.lax.top_k(tmp_scores, TOP_K)
            topk_w = jnp.take_along_axis(sfc, topk_idx, axis=-1)
            topk_w = topk_w / (topk_w.sum(axis=-1, keepdims=True) + 1e-20)
            return (topk_idx, topk_w * ROUTED_SCALE)
        B, N, H = x.shape
        xf = x.reshape(-1, H)
        topk_idx, topk_w = _gate(xf, gate_w, gate_bias)
        g = jax.nn.silu(jnp.einsum('th,ehi->tei', xf, w_gate))
        u = jnp.einsum('th,ehi->tei', xf, w_up)
        experts_y = jnp.einsum('tei,eih->teh', g * u, w_down)
        masked_y = jnp.take_along_axis(experts_y, topk_idx[:, :, None], axis=1)
        y = jnp.einsum('tkh,tk->th', masked_y, topk_w.astype(x.dtype)).reshape(B, N, H)
        shared = jax.nn.silu(x @ sw_gate) * (x @ sw_up) @ sw_down
        return y + shared

    def _L1_attn_ref(x, Wq, Wk, Wv):
        import jax, jax.numpy as jnp
        import numpy as np
        HEADS = 16
        C, T, E = x.shape
        H = HEADS
        D = E // H
        xr = x.reshape(C, T, H, D)
        q = jnp.einsum('cthd,ed->cthe', xr, Wq)
        k = jnp.einsum('cthd,ed->cthe', xr, Wk)
        v = jnp.einsum('cthd,ed->cthe', xr, Wv)
        diag_scores = jnp.einsum('cthd,cthd->cth', q, k) / jnp.sqrt(jnp.asarray(E, x.dtype))
        probs = jax.nn.softmax(diag_scores, axis=0)
        vsum = v.sum(axis=1)
        attn = probs[..., None] * vsum[:, None, :, :]
        return attn.reshape(C, T, E)

    def _L1_ffn_ref(hidden_states, w_red, wg, w1, b1, w2, b2):
        import jax, jax.numpy as jnp
        import numpy as np
        E, D, F, GATE_DIM = (8, 128, 512, 16)
        B, T = (2, 256)
        b, t, c = hidden_states.shape
        x = hidden_states.reshape(-1, c)
        red = x @ w_red
        wg_n = wg / jnp.maximum(jnp.linalg.norm(wg, axis=1, keepdims=True), 0.0001)
        logits = red @ wg_n.T
        gates = jax.nn.softmax(logits, axis=1)
        idx = jnp.argmax(gates, axis=1)
        scores = jnp.take_along_axis(gates, idx[:, None], axis=1)
        h = jax.nn.gelu(jnp.einsum('td,edf->etf', x, w1) + b1[:, None, :], approximate=False)
        y = jnp.einsum('etf,efd->etd', h, w2) + b2[:, None, :]
        out = jnp.take_along_axis(y, idx[None, :, None], axis=0)[0]
        out = out * scores
        return out.reshape(b, t, c)
    x = L0_attn_hidden_states
    xn = _layernorm(x, axis=-1)
    x = x + _L0_attn_ref(xn, L0_attn_Wq, L0_attn_Wk, L0_attn_Wv, L0_attn_Wo) + _L0_ffn_ref(xn, L0_ffn_gate_w, L0_ffn_gate_bias, L0_ffn_w_gate, L0_ffn_w_up, L0_ffn_w_down, L0_ffn_sw_gate, L0_ffn_sw_up, L0_ffn_sw_down)
    xn = _layernorm(x, axis=-1)
    x = x + _L1_attn_ref(xn, L1_attn_Wq, L1_attn_Wk, L1_attn_Wv) + _L1_ffn_ref(xn, L1_ffn_w_red, L1_ffn_wg, L1_ffn_w1, L1_ffn_b1, L1_ffn_w2, L1_ffn_b2)
    return x

_drawn_inputs = setup_inputs


def setup_inputs(seed=0):
    import zlib

    import numpy as np

    out = dict(_drawn_inputs(seed))
    spreads = {}
    factors = {'L0_ffn_gate_w': 8.0,
     'L0_ffn_gate_bias': 8.0,
     'L0_ffn_w_gate': 7.749,
     'L0_ffn_w_up': 7.702,
     'L0_ffn_w_down': 7.671,
     'L0_ffn_sw_gate': 7.369,
     'L0_ffn_sw_up': 6.781,
     'L0_ffn_sw_down': 8.0,
     'L1_ffn_w_red': 8.0,
     'L1_ffn_wg': 8.0,
     'L1_ffn_w1': 8.0,
     'L1_ffn_b1': 23.5,
     'L1_ffn_w2': 8.0,
     'L1_ffn_b2': 60.076}
    for name, (base, spread) in spreads.items():
        noise = np.random.default_rng([zlib.crc32(name.encode()), seed]).standard_normal(out[name].shape)
        drawn = base * np.exp(spread * noise) if base else spread * noise
        out[name] = jnp.asarray(drawn.astype(out[name].dtype))
    for name, factor in factors.items():
        out[name] = (out[name] * factor).astype(out[name].dtype)
    return out
```

```python
import concourse.bass as bass
from concourse import mybir
from contextlib import ExitStack

F32 = mybir.dt.float32
BF16 = mybir.dt.bfloat16
I32 = mybir.dt.int32
U32 = mybir.dt.uint32
ALU = mybir.AluOpType
ACT = mybir.ActivationFunctionType
AX = mybir.AxisListType

P = 128
B, L, D = 4, 512, 128
TB = L // P
NT = B * TB
T = B * L
H = 16
FEAT = 16
HD = D // H
E = 8
EI = 64
NJ = E * EI // P + 1
F1 = 512
NF = F1 // P
E1 = 8
GATE = 16
CAP = T
U = 4
NS = T // P + E1 - 1
XROWS = E1 * CAP + (E1 - 1) * P
YROWS = T + NS * P
NO_TOKEN = 1.0e6
XW = D + 2
COL_ID = D
COL_SCORE = D + 1
ROUTES = ((0, 3 * TB), (3 * TB, NT))
LN_EPS = 1e-5
ATTN_EPS = 1e-12
SPLIT_Q = (0, 0, 1, 1, 0, 2, 1, 2)
SPLIT_K = (0, 1, 0, 1, 2, 0, 2, 1)
NC = len(SPLIT_Q)
VW = HD + 1
QUAD = 32
A_SLOTS = 3
AV_LAG = 2
SLOT_SCORE = 2


def groups():
    return [(b, hg, i) for b in range(B) for hg in range(H // 4) for i in range(TB)]


def plan_work():
    out = [("xt", 0), ("q", 0), ("q", 1), ("k", 0), ("k", 1), ("v", 0)]
    qk = lambda b: [("q", 2 * b), ("q", 2 * b + 1), ("k", 2 * b), ("k", 2 * b + 1), ("v", b)]
    ffn = lambda b: [(s, NJ * b + j) for j in range(NJ) for s in ("g", "u")]
    weigh = lambda b: [("wt", b)] + [("w", (NJ - 1) * b + j) for j in range(NJ - 1)]
    finish = lambda b: [("n", 2 * b), ("n", 2 * b + 1), ("at", b), ("o", b)]
    out += [("xt", 1), ("xt", 2), ("xt", 3), ("lg", 0)] + qk(1) + ffn(0)
    both = lambda b: finish(b - 1)[:2] + weigh(b)[:2] + finish(b - 1)[2:3] + weigh(b)[2:] + finish(b - 1)[3:]
    turn = lambda b: [("x2", b), ("d", 2 * b), ("d", 2 * b + 1)]
    fill = [weigh(0) + [("cw", 0)] + ffn(1) + qk(2) + [("cm", 0)], both(1) + ffn(2) + turn(0) + qk(3),
            both(2) + ffn(3) + turn(1), both(3) + turn(2) + [("ra", 0), ("rk", 0)]]
    g = groups()
    for n in range(len(g) + AV_LAG):
        if n < len(g):
            out += [("s", 2 * n), ("s", 2 * n + 1)]
        if n >= AV_LAG:
            out.append(("av", n - AV_LAG))
        b, at = divmod(n, 4 * TB)
        if b < B:
            f = fill[b]
            out += f[len(f) * max(at - 1, 0) // 15:len(f) * at // 15]
    out += finish(B - 1) + turn(B - 1) + [("ra", 1), ("rk", 1), ("vb", 0)]
    return out


def two_layers(nc, x_in, wq_t, wk_t, wv_t, wo_t, gate_w, gate_bias, w_gate, w_up, w_down, sw_gate, sw_up,
               sw_down, head_wq, head_wk, head_wv_t, w_red_t, wg, w1, b1, w2, b2, out):
    plan = plan_work()
    RING_KINDS = ("xt", "q", "k", "v", "lg", "g", "u", "wt", "w", "n", "at", "o",
                  "cw", "cm", "x2", "d", "rk", "vb")
    place = {item: k for k, item in enumerate(it for it in plan if it[0] in RING_KINDS)}
    RING = 3

    with ExitStack() as ctx:
        def sb(name, shape, dt=F32):
            return ctx.enter_context(nc.sbuf_tensor(name, shape, dt))

        def ps(name, shape):
            return ctx.enter_context(nc.psum_tensor(name, shape, F32))

        def sem(name):
            return ctx.enter_context(nc.semaphore(name))

        X = sb("X", [P, NT, D])
        XN = sb("XN", [P, NT, XW])
        XNT = sb("XNT", [P, T])
        WQ = sb("WQ", [P, H * FEAT])
        WK = sb("WK", [P, H * FEAT])
        WV = sb("WV", [P, D])
        WO = sb("WO", [P, D])
        GW = sb("GW", [P, E])
        GB = sb("GB", [P, E])
        WG = sb("WG", [P, NJ * P])
        WU = sb("WU", [P, NJ * P])
        WD = sb("WD", [P, NJ, D])
        IDF = sb("IDF", [P, P])
        IDB = sb("IDB", [P, P], BF16)
        TRI = sb("TRI", [P, P])
        ONES = sb("ONES", [P, P])
        SEL = sb("SEL", [P, 36])
        SELW = sb("SELW", [3 * E, NJ - 1, P], BF16)
        LOW = sb("LOW", [P, E, E])
        CNT = sb("CNT", [P, TB])
        NHALF = sb("NHALF", [P, NT])
        NROOT = sb("NROOT", [E, 1])
        STATS = sb("STATS", [P, NT, 6])
        MV = sb("MV", [P, NT, 2])
        VE = sb("VE", [P, NT])
        RSTD = sb("RSTD", [P, NT])
        PARTS = sb("PARTS", [P, 3, 3, L], BF16)
        REST = sb("REST", [P, L])
        STK = [sb(f"STK{n}", [P, 2, H, L], BF16) for n in range(2)]
        VH = sb("VH", [P, 3, TB, H, VW])
        VP = sb("VP", [P, 2, 2, H, HD])
        A = sb("A", [P, A_SLOTS, 4, L])
        YS = sb("YS", [P, 4, L])
        DEN = sb("DEN", [P, H])
        RDEN = sb("RDEN", [P, H])
        AO = sb("AO", [P, TB, D])
        AOT = sb("AOT", [P, L])
        SG = sb("SG", [P, 2, L])
        G = sb("G", [P, 2, L])
        HT = sb("HT", [P, 2, NJ, L])
        WTS = sb("WTS", [3 * E, L], BF16)
        SFC = sb("SFC", [P, NT, E])
        GS = sb("GS", [P, NT, 4])
        CMP = A[:, 0, 0:2, :].rearrange("p a n -> p (a n)")
        EQ = A[:, 1, 0:2, :].rearrange("p a n -> p (a n)")
        RANK = sb("RANK", [P, NT, E])
        MASKED = sb("MASKED", [P, NT, E])
        WSUM = sb("WSUM", [P, NT])
        WPART = sb("WPART", [P, NT, 3, E], BF16)

        W8 = sb("W8", [HD, 3 * HD])
        WGN = sb("WGN", [E1, GATE])
        WGSQ = sb("WGSQ", [E1, GATE])
        WGNORM = sb("WGNORM", [E1, 1])
        REDT = sb("REDT", [GATE, P])
        WGNT = sb("WGNT", [GATE, E1])
        REPL = sb("REPL", [HD, P])
        BDMASK = sb("BDMASK", [P, P])
        REP3 = sb("REP3", [P, 3 * HD])
        BDQ = sb("BDQ", [P, P])
        BDK = sb("BDK", [P, P])
        BDV = sb("BDV", [P, P])
        BDR = sb("BDR", [P, P + E1])
        INIT = sb("INIT", [P, XW])
        XS = sb("XS", [P, B])
        PADROW = sb("PADROW", [P, NS])
        ROW = [sb(f"ROW{n}", [P, 1], U32) for n in range(U)]
        SCORE = [sb(f"SCORE{n}", [P, 1]) for n in range(U)]
        DS = sb("DS", [P, NT, H])
        LG = sb("LG", [P, NT, E1])
        MX = sb("MX", [P, NT])
        PRI = sb("PRI", [P, E1])
        OH = sb("OH", [P, NT, E1])
        PFX = sb("PFX", [P, NT, E1])
        EXC = sb("EXC", [P, NT, E1])
        EBASE = sb("EBASE", [P, E1])
        POS = sb("POS", [P, NT], U32)
        SLOTI = sb("SLOTI", [1, NS])
        CNTI = sb("CNTI", [1, E1], I32)
        CNTF = sb("CNTF", [1, E1])
        INCL = sb("INCL", [1, E1])
        STAB = sb("STAB", [1, 4, NS])
        SEXP = sb("SEXP", [1, NS], I32)
        SBASE = sb("SBASE", [1, NS], I32)
        JUNK = sb("JUNK", [P, 1])
        SMX = sb("SMX", [P, TB * H])
        W1 = STK[0][:, 0].rearrange("p h t -> p (h t)").bitcast(F32)
        W2 = STK[0][:, 1].rearrange("p h t -> p (h t)").bitcast(F32)
        B1 = STK[1][:, 0].rearrange("p h t -> p (h t)").bitcast(F32)
        B2 = STK[1][:, 1, 0:4].rearrange("p h t -> p (h t)").bitcast(F32)
        HB = [A[:, 0, n] for n in range(2)]
        GE = [A[:, 0, 2 + n] for n in range(2)]
        GT = [A[:, 1, n] for n in range(2)]
        XTS = [A[:, 1, 2, n * P:(n + 1) * P] for n in range(2)]
        YO = [A[:, 1, 3, n * P:(n + 1) * P] for n in range(2)]
        XSL = [A[:, 2, n, 0:XW] for n in range(U)]
        YG = HT[:, 0, 0:4].rearrange("p j t -> p (j t)").rearrange("p (t d) -> p t d", d=D)
        RUN = MASKED
        BDVS = HT[:, 0, 0].rearrange("p (b d) -> p b d", b=B)
        VBC = AO
        ATT = REST

        xs_dram = nc.dram_tensor("xs_dram", [XROWS, XW], F32, kind="Internal").ap()
        y_dram = nc.dram_tensor("y_dram", [YROWS, D], F32, kind="Internal").ap()
        parts_dram = nc.dram_tensor("parts_dram", [B, 2, 3, H, FEAT, L], BF16, kind="Internal").ap()

        SC = ps("SC", [P, 4, L])
        YT = ps("YT", [P, L])
        WB = [ps(f"WB{r}", [P, L]) for r in range(RING)]

        DOWN = [WB[2][:, 0:P], YT[:, 0:P]]

        x_loaded = [sem(f"x_loaded{b}") for b in range(B)]
        qkv_w_loaded = sem("qkv_w_loaded")
        ffn_w_loaded = sem("ffn_w_loaded")
        const_ready = sem("const_ready")
        ones_ready = sem("ones_ready")
        var_ready = sem("var_ready")
        rstd_ready = sem("rstd_ready")
        xn_ready = sem("xn_ready")
        work_ready = [sem(f"work_ready{r}") for r in range(RING)]
        work_used = [sem(f"work_used{r}") for r in range(RING)]
        first_part = sem("first_part")
        sig_ready = sem("sig_ready")
        parts_ready = sem("parts_ready")
        parts_saved = [sem(f"parts_saved{n}") for n in range(3)]
        stack_loaded = [sem(f"stack_loaded{n}") for n in range(2)]
        score_ready = [sem(f"score_ready{n}") for n in range(2)]
        squared = sem("squared")
        masked = sem("masked")
        av_done = sem("av_done")
        yt_cleared = sem("yt_cleared")
        yt_saved = sem("yt_saved")
        v_prefix = sem("v_prefix")
        routed = sem("routed")
        small_w_loaded = sem("small_w_loaded")
        w12_loaded = sem("w12_loaded")
        b12_loaded = sem("b12_loaded")
        consts1 = sem("consts1")
        sumsq_ready = sem("sumsq_ready")
        norm_ready = sem("norm_ready")
        wgn_ready = sem("wgn_ready")
        init_ready = sem("init_ready")
        xs_cleared = sem("xs_cleared")
        logits_centred = sem("logits_centred")
        logits_exped = sem("logits_exped")
        choice_ready = sem("choice_ready")
        pos_ready = sem("pos_ready")
        xs_scattered = sem("xs_scattered")
        slots_ready = sem("slots_ready")
        bdvs_ready = sem("bdvs_ready")
        diag_centred = sem("diag_centred")
        diag_exped = sem("diag_exped")
        xs_loaded = [sem(f"xs_loaded{n}") for n in range(U)]
        ids_kept = sem("ids_kept")
        x_turned = sem("x_turned")
        xt_copied = sem("xt_copied")
        up_done = sem("up_done")
        biased = sem("biased")
        gelu_done = sem("gelu_done")
        g_turned = sem("g_turned")
        gt_copied = sem("gt_copied")
        down_done = sem("down_done")
        y_summed = sem("y_summed")
        y_ready = sem("y_ready")
        y_scatter_begun = sem("y_scatter_begun")
        y_scattered = [sem(f"y_scattered{n}") for n in range(2)]
        y_loaded = [sem(f"y_loaded{b}") for b in range(B)]
        out_ready = sem("out_ready")
        saved = sem("saved")
        dve_seq = sem("dve_seq")
        pool_seq = sem("pool_seq")

        block = ctx.enter_context(nc.Block())

        def bank(item):
            return WB[place[item] % RING]

        def wait_bank(eng, item):
            k = place[item]
            if k >= RING:
                eng.wait_ge(work_used[k % RING], k // RING)

        def wait_made(eng, item):
            k = place[item]
            eng.wait_ge(work_ready[k % RING], k // RING + 1)

        def made(ins, item):
            ins.then_inc(work_ready[place[item] % RING], 1)

        def wait_used(eng, item):
            k = place[item]
            eng.wait_ge(work_used[k % RING], k // RING + 1)

        def used(ins, item):
            ins.then_inc(work_used[place[item] % RING], 1)

        def blk_of(kind, n):
            b, blk = divmod(n, 2)
            return b, int(kind == "k"), blk, 4 * b + 2 * int(kind == "k") + blk

        def inside(s):
            return not isinstance(s, int) or 0 <= s < NS

        def at_least(eng, semaphore, v):
            if not isinstance(v, int) or v > 0:
                eng.wait_ge(semaphore, v)

        def loaded(s, u):
            return 16 // U * s + (16 - 16 // U * (u % U))

        def run_slots(eng, step, end):
            full = (NS - 1) // U
            for s in range(U):
                step(s, s)
            with eng.Fori(1, full) as m:
                for u in range(U):
                    step(m * U + u, u)
            for s in range(full * U, end):
                step(s, s % U)

        xt_in = x_in.rearrange("b (i p) d -> b p i d", p=P)
        xt_out = out.rearrange("b (i p) d -> b p i d", p=P)

        @block.sync
        def _(sp):
            for b in range(B):
                sp.dma_start(X[:, b * TB:(b + 1) * TB, :], xt_in[b]).then_inc(x_loaded[b], 16)
                if b == 0:
                    sp.dma_start(WQ[:], wq_t).then_inc(qkv_w_loaded, 16)
                    sp.dma_start(WK[:], wk_t).then_inc(qkv_w_loaded, 16)
            for b in range(B):
                for n in range(4 * b, 4 * b + 4):
                    qk, blk = (n % 4) // 2, n % 2
                    sp.wait_ge(parts_ready, n + 1)
                    dst = parts_dram[b, qk, :, 8 * blk:8 * blk + 8].rearrange("c h d t -> (h d) c t")
                    sp.dma_start(dst, PARTS[:, n % 3]).then_inc(parts_saved[n % 3], 16)
                for n in range(4 * b + 1, 4 * b + 4):
                    sp.wait_ge(parts_saved[n % 3], 16 * (n // 3 + 1))
                if b >= 2:
                    for half in range(2):
                        sp.wait_ge(score_ready[half], 16 * (b - 1))
                if b == 2:
                    sp.wait_ge(init_ready, 1)
                    rows = xs_dram.rearrange("(j p) c -> p j c", p=P)
                    sp.dma_start(rows, INIT[:].rearrange("p (o c) -> p o c", o=1)
                                 .to_broadcast([P, XROWS // P, XW])).then_inc(xs_cleared, 16)
                for c in range(NC):
                    for qk, parts in ((0, SPLIT_Q), (1, SPLIT_K)):
                        src = parts_dram[b, qk, parts[c]].rearrange("h d t -> d h t")
                        sp.dma_start(STK[b % 2][FEAT * c:FEAT * (c + 1), qk], src).then_inc(stack_loaded[b % 2], 16)
            sp.wait_ge(score_ready[0], 4 * TB * 3)
            sp.wait_ge(score_ready[1], 4 * TB * 3)
            sp.dma_start(W1.rearrange("p (e f) -> p e f", e=E1), w1.rearrange("e d f -> d e f")).then_inc(w12_loaded, 16)
            sp.dma_start(W2.rearrange("p (e k d) -> p e k d", e=E1, k=NF),
                         w2.rearrange("e (k p) d -> p e k d", p=P)).then_inc(w12_loaded, 16)
            sp.wait_ge(score_ready[0], 4 * TB * 4)
            sp.wait_ge(score_ready[1], 4 * TB * 4)
            sp.dma_start(B1, b1.rearrange("(o e) f -> o (e f)", o=1).to_broadcast([P, E1 * F1])).then_inc(b12_loaded, 16)
            sp.dma_start(B2, b2.rearrange("(o e) f -> o (e f)", o=1).to_broadcast([P, E1 * D])).then_inc(b12_loaded, 16)
            sp.wait_ge(slots_ready, 2)
            sp.wait_ge(xs_scattered, 16 * NT)

            def load_slot(s, u):
                at_least(sp, x_turned, s - U + 1)
                at_least(sp, ids_kept, s - U + 1)
                row = sp.value_load(SBASE[0:1, bass.ds(s, 1)], min_val=0, max_val=XROWS - P)
                sp.dma_start(XSL[u], xs_dram[bass.ds(row, P), :]).then_inc(xs_loaded[u], 16)

            run_slots(sp, load_slot, NS)
            for n in range(2):
                sp.wait_ge(y_scattered[n], 16 * ((NS + 1 - n) // 2))
            y_tok = y_dram[0:T].rearrange("(b i p) d -> b p i d", b=B, p=P)
            for b in range(B):
                sp.dma_start(YG[:, b * TB:(b + 1) * TB], y_tok[b]).then_inc(y_loaded[b], 16)
            for b in range(B):
                sp.wait_ge(out_ready, b + 1)
                sp.dma_start(xt_out[b], X[:, b * TB:(b + 1) * TB, :]).then_inc(saved, 16)
            sp.wait_ge(saved, 16 * B)

        @block.gpsimd
        def _(pool):
            n_seq = 0

            def seq(ins):
                nonlocal n_seq
                n_seq += 1
                ins.then_inc(pool_seq, 1)
                pool.wait_ge(pool_seq, n_seq)

            seq(pool.memset(IDF[:], 0.0))
            pool.affine_select(out=IDF[:], in_=IDF[:], pattern=[[-1, P]], compare_op=ALU.not_equal,
                               fill=1.0, base=0, channel_multiplier=1).then_inc(const_ready, 1)
            seq(pool.memset(NHALF[:], -0.5))
            pool.memset(VH[:, :, :, :, HD:HD + 1], 1.0).then_inc(ones_ready, 1)

            def rstd(m):
                pool.wait_ge(var_ready, m + 1)
                r = slice(m % B * TB, (m % B + 1) * TB)
                pool.tensor_tensor(RSTD[:, r], VE[:, r], NHALF[:, r], ALU.pow).then_inc(rstd_ready, 1)

            for b in range(B):
                rstd(b)
            pool.memset(ONES[:], 1.0)
            seq(pool.memset(TRI[:], 1.0))
            seq(pool.affine_select(out=TRI[:], in_=TRI[:], pattern=[[1, P]], compare_op=ALU.is_ge,
                                   fill=0.0, base=0, channel_multiplier=-1))
            seq(pool.memset(IDB[:], 0.0))
            seq(pool.affine_select(out=IDB[:], in_=IDB[:], pattern=[[-1, P]], compare_op=ALU.not_equal,
                                   fill=1.0, base=0, channel_multiplier=1))
            seq(pool.memset(SEL[:], 0.0))
            v = SEL[:, 0:32].rearrange("p (h e) -> p h e", h=4)
            pool.affine_select(out=v, in_=v, pattern=[[-QUAD, 4], [-1, HD]], compare_op=ALU.not_equal,
                               fill=1.0, base=0, channel_multiplier=1)
            seq(pool.affine_select(out=SEL[:, 32:36], in_=SEL[:, 32:36], pattern=[[-QUAD, 4]],
                                   compare_op=ALU.not_equal, fill=1.0, base=-HD, channel_multiplier=1))
            seq(pool.memset(LOW[:], 1.0))
            seq(pool.affine_select(out=LOW[:], in_=LOW[:], pattern=[[1, E], [-1, E]], compare_op=ALU.is_gt,
                                   fill=0.0, base=0, channel_multiplier=0))
            seq(pool.memset(SELW[:], 0.0))
            v = SELW[:].rearrange("k j (e f) -> k j e f", e=2)
            for c in range(3):
                seq(pool.affine_select(out=v, in_=v, pattern=[[-2, NJ - 1], [-1, 2], [0, EI]],
                                       compare_op=ALU.not_equal, fill=1.0, base=-E * c, channel_multiplier=1))
            pool.iota(CNT[:], [[P, TB]], base=1, channel_multiplier=1,
                      allow_small_or_imprecise_dtypes=True).then_inc(const_ready, 1)
            seq(pool.memset(REPL[:], 0.0))
            v = REPL[:].rearrange("p (h e) -> p h e", h=H)
            pool.affine_select(out=v, in_=v, pattern=[[0, H], [-1, HD]], compare_op=ALU.not_equal,
                               fill=1.0, base=0, channel_multiplier=1)
            seq(pool.memset(BDMASK[:], 1.0))
            v = BDMASK[:].rearrange("p (h e) -> p h e", h=H)
            seq(pool.affine_select(out=v, in_=v, pattern=[[-HD, H], [0, HD]], compare_op=ALU.is_ge,
                                   fill=0.0, base=0, channel_multiplier=1))
            seq(pool.affine_select(out=v, in_=v, pattern=[[HD, H], [0, HD]], compare_op=ALU.is_ge,
                                   fill=0.0, base=HD - 1, channel_multiplier=-1))
            pool.iota(PRI[:], [[-1, E1]], base=E1, channel_multiplier=0, allow_small_or_imprecise_dtypes=True)
            pool.iota(EBASE[:], [[CAP, E1]], base=-1, channel_multiplier=0, allow_small_or_imprecise_dtypes=True)
            seq(pool.iota(SLOTI[:], [[1, NS]], base=0, channel_multiplier=0, allow_small_or_imprecise_dtypes=True))
            pool.iota(PADROW[:], [[P, NS]], base=T, channel_multiplier=1, allow_small_or_imprecise_dtypes=True)
            seq(pool.memset(INIT[:], 0.0))
            pool.memset(INIT[:, COL_ID:COL_ID + 1], NO_TOKEN).then_inc(init_ready, 1)
            seq(pool.iota(XN[:, :, COL_ID:COL_ID + 1], [[P, NT], [1, 1]], base=0, channel_multiplier=1,
                          allow_small_or_imprecise_dtypes=True))
            seq(pool.memset(NROOT[:], 0.5))
            pool.nop().then_inc(consts1, 1)
            pool.wait_ge(sumsq_ready, 1)
            pool.tensor_tensor(WGNORM[:], WGNORM[:], NROOT[:], ALU.pow).then_inc(norm_ready, 1)

            def scatter(r):
                lo, hi = ROUTES[r]
                pool.wait_ge(pos_ready, r + 1)
                if r == 0:
                    pool.wait_ge(xs_cleared, 16)
                for t in range(lo, hi):
                    pool.indirect_dma_start(out=xs_dram[:, :], out_offset=bass.IndirectOffsetOnAxis(ap=POS[:, t:t + 1], axis=0),
                                            in_=XN[:, t], in_offset=None).then_inc(xs_scattered, 16)

            for kind, n in plan:
                if kind == "x2":
                    rstd(B + n)
                if kind == "rk":
                    scatter(n)
                if kind == "s":
                    pool.wait_ge(squared, n + 1)
                    g = n // 2
                    a = A[:, g % A_SLOTS, 2 * (n % 2):2 * (n % 2) + 2, 0:P]
                    pool.affine_select(out=a, in_=a, pattern=[[0, 2], [1, P]], compare_op=ALU.is_ge,
                                       fill=0.0, base=0, channel_multiplier=-1).then_inc(masked, 1)
                if kind == "s" and n % (8 * TB) == 0:
                    b = n // (8 * TB)
                    wait_used(pool, ("v", b))
                    if b >= 2:
                        wait_made(pool, ("n", 2 * (b - 2) + 1))
                    vb = VH[:, b % 3, :, :, 0:HD]
                    seq(pool.tensor_tensor(VP[:, b % 2, 0], vb[:, 0], vb[:, 1], ALU.add))
                    pool.tensor_tensor(VP[:, b % 2, 1], VP[:, b % 2, 0], vb[:, 2], ALU.add).then_inc(v_prefix, 1)

            def scatter_y(s, u):
                at_least(pool, y_ready, s + 1)
                pool.sem_inc(y_scatter_begun, 1)
                pool.indirect_dma_start(out=y_dram[:, :],
                                        out_offset=bass.IndirectOffsetOnAxis(ap=ROW[u][:], axis=0),
                                        in_=YO[u % 2], in_offset=None).then_inc(y_scattered[u % 2], 16)

            run_slots(pool, scatter_y, NS)

        @block.scalar
        def _(act):
            act.dma_start(WV[:], wv_t).then_inc(qkv_w_loaded, 16)
            act.dma_start(GW[:], gate_w).then_inc(ffn_w_loaded, 16)
            act.dma_start(GB[:], gate_bias.rearrange("(a e) -> a e", a=1).to_broadcast([P, E])).then_inc(ffn_w_loaded, 16)
            nr = (NJ - 1) * P
            act.dma_start(WG[:, 0:nr].rearrange("h (e i) -> h e i", e=E),
                          w_gate.rearrange("e h i -> h e i")).then_inc(ffn_w_loaded, 16)
            act.dma_start(WG[:, nr:], sw_gate).then_inc(ffn_w_loaded, 16)
            act.dma_start(WU[:, 0:nr].rearrange("h (e i) -> h e i", e=E),
                          w_up.rearrange("e h i -> h e i")).then_inc(ffn_w_loaded, 16)
            act.dma_start(WU[:, nr:], sw_up).then_inc(ffn_w_loaded, 16)
            act.dma_start(WD[:, 0:NJ - 1], w_down.rearrange("(j e) i h -> (e i) j h", e=2)).then_inc(ffn_w_loaded, 16)
            act.dma_start(WD[:, NJ - 1], sw_down).then_inc(ffn_w_loaded, 16)
            act.dma_start(WO[:], wo_t).then_inc(ffn_w_loaded, 16)
            act.dma_start(W8[:, 0:HD], head_wq).then_inc(small_w_loaded, 16)
            act.dma_start(W8[:, HD:2 * HD], head_wk).then_inc(small_w_loaded, 16)
            act.dma_start(W8[:, 2 * HD:], head_wv_t).then_inc(small_w_loaded, 16)
            act.dma_start(REDT[:], w_red_t).then_inc(small_w_loaded, 16)
            act.dma_start(WGN[:], wg).then_inc(small_w_loaded, 16)

            for kind, n in plan:
                item = (kind, n)
                if kind == "xt":
                    wait_made(act, item)
                    used(act.copy(XNT[:, n * L:(n + 1) * L], bank(item)[:]), item)
                if kind in "qk":
                    s = blk_of(kind, n)[3]
                    wait_made(act, item)
                    if s >= 3:
                        act.wait_ge(parts_saved[s % 3], 16 * (s // 3))
                    act.copy(PARTS[:, s % 3, 0], bank(item)[:]).then_inc(first_part, 1)
                if kind == "v":
                    wait_made(act, item)
                    act.wait_ge(ones_ready, 1)
                    if n >= 3:
                        wait_made(act, ("n", 2 * (n - 3) + 1))
                    used(act.copy(VH[:, n % 3, :, :, 0:HD],
                                  bank(item)[:].rearrange("p (i h e) -> p i h e", i=TB, h=H)), item)
                if kind == "lg":
                    wait_made(act, item)
                    used(act.activation(SFC[:], bank(item)[:, 0:NT * E].rearrange("p (t e) -> p t e", e=E),
                                        ACT.Sigmoid), item)
                if kind == "g":
                    wait_made(act, item)
                    if n >= 2:
                        wait_used(act, ("g", n - 2))
                    act.activation(SG[:, n % 2], bank(item)[:], ACT.Sigmoid).then_inc(sig_ready, 1)
                if kind == "s":
                    g, half = divmod(n, 2)
                    w = L - P * (g % TB)
                    act.wait_ge(score_ready[half], g + 1)
                    if g >= A_SLOTS:
                        act.wait_ge(av_done, g - A_SLOTS + 1)
                    act.activation(A[:, g % A_SLOTS, 2 * half:2 * half + 2, 0:w], SC[:, 2 * half:2 * half + 2, 0:w],
                                   ACT.Square, bias=1.0, scale=0.25).then_inc(squared, 1)
                if kind == "at":
                    wait_made(act, item)
                    if n >= 1:
                        wait_made(act, ("o", n - 1))
                    used(act.copy(AOT[:], bank(item)[:]), item)
                if kind == "x2":
                    wait_made(act, item)
                    used(act.activation(XNT[:, n * L:(n + 1) * L], bank(item)[:], ACT.Identity,
                                        accum_out=XS[:, n:n + 1]), item)
                if kind == "ra":
                    lo, hi = ROUTES[n]
                    act.wait_ge(logits_centred, n + 1)
                    act.activation(EXC[:, lo:hi], EXC[:, lo:hi], ACT.Exp).then_inc(logits_exped, 1)
                if kind == "vb":
                    wait_made(act, item)
                    used(act.copy(VBC[:].rearrange("p b d -> p (b d)"), bank(item)[:]), item)

            act.wait_ge(diag_centred, 1)
            act.activation(DS[:], DS[:], ACT.Exp, scale=D ** -0.5).then_inc(diag_exped, 1)

            def act_step(st, u):
                if inside(st):
                    at_least(act, biased, st + 1)
                    at_least(act, g_turned, st - 1)
                    act.activation(GE[u % 2], HB[u % 2], ACT.Gelu).then_inc(gelu_done, 1)
                if inside(st + 1):
                    copy_x(st + 1, u + 1)

            def copy_x(s, u):
                at_least(act, x_turned, s + 1)
                at_least(act, up_done, s - 1)
                act.copy(XTS[u % 2], WB[u % 2][:, 0:P]).then_inc(xt_copied, 1)

            act.wait_ge(slots_ready, 2)
            copy_x(0, 0)
            run_slots(act, act_step, NS)

        @block.tensor
        def _(pe):
            for kind, n in plan:
                item = (kind, n)
                if kind in RING_KINDS:
                    wait_bank(pe, item)
                    w = bank(item)
                if kind == "xt":
                    if n == 0:
                        pe.wait_ge(const_ready, 1)
                    pe.wait_ge(xn_ready, n + 1)
                    for i in range(TB):
                        last = pe.transpose(w[:, i * P:(i + 1) * P], XN[:, n * TB + i, 0:D], IDF[:])
                if kind in "qk":
                    b, qk, blk, s = blk_of(kind, n)
                    if s == 0:
                        pe.wait_ge(qkv_w_loaded, 48)
                    wait_used(pe, ("xt", b))
                    last = pe.matmul(w[:], (WQ, WK)[qk][:, blk * P:(blk + 1) * P], XNT[:, b * L:(b + 1) * L],
                                     start=True, stop=True)
                if kind == "v":
                    wait_used(pe, ("xt", n))
                    for i in range(TB):
                        t = n * TB + i
                        last = pe.matmul(w[:, i * P:(i + 1) * P], XNT[:, t * P:(t + 1) * P], WV[:],
                                         start=(i == 0), stop=True, skip_group_check=True)
                if kind == "lg":
                    pe.wait_ge(ffn_w_loaded, 144)
                    for b in range(B):
                        wait_used(pe, ("xt", b))
                    for t in range(NT):
                        last = pe.matmul(w[:, t * E:(t + 1) * E], XNT[:, t * P:(t + 1) * P], GW[:],
                                         start=(t == 0), stop=True, skip_group_check=True)
                if kind in "gu":
                    b, j = divmod(n, NJ)
                    last = pe.matmul(w[:], (WG if kind == "g" else WU)[:, j * P:(j + 1) * P],
                                     XNT[:, b * L:(b + 1) * L], start=True, stop=True)
                if kind == "wt":
                    if n == 0:
                        pe.wait_ge(routed, 1)
                        pe.wait_ge(const_ready, 2)
                    for i in range(TB):
                        last = pe.transpose(w[0:3 * E, 0:L // 2].bitcast(BF16)[:, i * P:(i + 1) * P],
                                            WPART[:, n * TB + i].rearrange("p c e -> p (c e)"), IDB[:])
                if kind == "w":
                    b, j = divmod(n, NJ - 1)
                    wait_used(pe, ("wt", b))
                    last = pe.matmul(w[:], SELW[:, j], WTS[:], start=True, stop=True)
                if kind == "s":
                    g, half = divmod(n, 2)
                    b, hg, i = groups()[g]
                    if g % (4 * TB) == 0 and half == 0:
                        pe.wait_ge(stack_loaded[b % 2], 16 * 2 * NC * (b // 2 + 1))
                    if g >= 1:
                        pe.wait_ge(squared, 2 * (g - 1) + half + 1)
                    for k in range(2):
                        h = 4 * hg + 2 * half + k
                        last = pe.matmul(SC[:, 2 * half + k, 0:L - P * i], STK[b % 2][:, 1, h, i * P:(i + 1) * P],
                                         STK[b % 2][:, 0, h, i * P:L], start=True, stop=True)
                    last.then_inc(score_ready[half], 1)
                if kind == "av":
                    b, hg, i = groups()[n]
                    pe.wait_ge(masked, 2 * n + 2)
                    if n == 0:
                        pe.wait_ge(yt_cleared, 1)
                    if i == 0 and n > 0:
                        pe.wait_ge(yt_saved, n // TB)
                    for k in range(4):
                        last = pe.matmul(YT[QUAD * k:QUAD * k + VW, i * P:L], VH[:, b % 3, i, 4 * hg + k],
                                         A[:, n % A_SLOTS, k, 0:L - P * i], start=(i == 0), stop=(i == TB - 1),
                                         skip_group_check=True)
                    last.then_inc(av_done, 1)
                if kind == "n":
                    b = n // 2
                    pe.wait_ge(yt_saved, 4 * (b + 1))
                    pe.wait_ge(v_prefix, b + 1)
                    for k in range(2):
                        i = 2 * (n % 2) + k
                        num = w[:, k * 144:(k + 1) * 144].rearrange("p (g c) -> p g c", g=4)[:, :, 0:32]\
                            .rearrange("p g (h e) -> p g h e", h=4)
                        vi = VH[:, b % 3, i, :, 0:HD].rearrange("p (g h) e -> p g h e", g=4)
                        pe.matmul(num, TRI[:], vi, start=(k == 0), stop=False, skip_group_check=True)
                        if i >= 1:
                            before = VH[:, b % 3, 0, :, 0:HD] if i == 1 else VP[:, b % 2, i - 2]
                            pe.matmul(num, ONES[:], before.rearrange("p (g h) e -> p g h e", g=4), start=False,
                                      stop=False, skip_group_check=True)
                        for hg in range(4):
                            last = pe.matmul(w[:, k * 144 + hg * 36:k * 144 + hg * 36 + 36],
                                             YS[:, hg, i * P:(i + 1) * P], SEL[:], start=False, stop=True,
                                             skip_group_check=True)
                if kind == "at":
                    wait_used(pe, ("n", 2 * n + 1))
                    for i in range(TB):
                        last = pe.transpose(w[:, i * P:(i + 1) * P], AO[:, i], IDF[:])
                if kind == "o":
                    wait_used(pe, ("at", n))
                    wait_used(pe, ("w", (NJ - 1) * n + NJ - 2))
                    wait_used(pe, ("u", NJ * n + NJ - 1))
                    for i in range(TB):
                        o = w[:, i * P:(i + 1) * P]
                        for j in range(NJ):
                            pe.matmul(o, HT[:, n % 2, j, i * P:(i + 1) * P], WD[:, j], start=(i == 0 and j == 0),
                                      stop=False, skip_group_check=True)
                        last = pe.matmul(o, AOT[:, i * P:(i + 1) * P], WO[:], start=False, stop=True,
                                         skip_group_check=True)
                if kind == "cw":
                    pe.wait_ge(small_w_loaded, 16 * 5)
                    pe.wait_ge(consts1, 1)
                    pe.wait_ge(wgn_ready, 1)
                    pe.matmul(w[:, 0:3 * HD], REPL[:], W8[:], start=True, stop=True)
                    last = pe.transpose(w[0:GATE, 3 * HD:3 * HD + E1], WGN[:], IDF[0:E1, 0:E1])
                if kind == "cm":
                    wait_used(pe, ("cw", 0))
                    pe.matmul(w[:, 0:P], BDQ[:], BDK[:], start=True, stop=True)
                    last = pe.matmul(w[:, P:P + E1], REDT[:], WGNT[:], start=False, stop=True, skip_group_check=True)
                if kind == "x2":
                    pe.wait_ge(xn_ready, B + n + 1)
                    for i in range(TB):
                        last = pe.transpose(w[:, i * P:(i + 1) * P], XN[:, n * TB + i, 0:D], IDF[:])
                if kind == "d":
                    wait_used(pe, ("x2", n // 2))
                    wait_used(pe, ("cm", 0))
                    for k in range(2):
                        t = 2 * n + k
                        last = pe.matmul(w[:, k * (P + E1):(k + 1) * (P + E1)], XNT[:, t * P:(t + 1) * P], BDR[:],
                                         start=(k == 0), stop=True, skip_group_check=True)
                if kind == "rk":
                    pe.wait_ge(choice_ready, n + 1)
                    lo, hi = ROUTES[n]
                    c = (hi - lo) * E1
                    pe.matmul(w[:, 0:c], TRI[:], OH[:, lo:hi], start=True, stop=False, skip_group_check=True)
                    last = pe.matmul(w[:, 0:c], ONES[:], RUN[:, lo:hi], start=False, stop=True, skip_group_check=True)
                    if hi == NT:
                        last = pe.matmul(w[:, 128:128 + E1], ONES[:], PFX[:, NT - 1], start=False, stop=True,
                                         skip_group_check=True)
                if kind == "vb":
                    pe.wait_ge(bdvs_ready, 1)
                    last = pe.matmul(w[:], ONES[:], BDVS.rearrange("p b d -> p (b d)"), start=True, stop=True)
                if kind in RING_KINDS:
                    made(last, item)

            def turn_x(s, u):
                at_least(pe, xs_loaded[u % U], loaded(s, u))
                at_least(pe, xt_copied, s - 1)
                pe.transpose(WB[u % 2][:, 0:P], XSL[u % U][:, 0:D], IDF[:]).then_inc(x_turned, 1)

            def pe_step(st, u):
                if inside(st):
                    e = pe.value_load(SEXP[0:1, bass.ds(st, 1)], min_val=0, max_val=E1 - 1)
                    at_least(pe, xt_copied, st + 1)
                    at_least(pe, biased, st - 1)
                    pe.matmul(SC[:, u % 2, :], XTS[u % 2], W1[:, bass.ds(e * F1, F1)], start=True,
                              stop=True).then_inc(up_done, 1)
                if inside(st - 1):
                    v = (u + 1) % 2
                    at_least(pe, gelu_done, st)
                    at_least(pe, gt_copied, st - 2)
                    for k in range(NF):
                        last = pe.transpose(SC[:, 2 + v, k * P:(k + 1) * P], GE[v][:, k * P:(k + 1) * P], IDF[:])
                    last.then_inc(g_turned, 1)
                if inside(st - 2):
                    e = pe.value_load(SEXP[0:1, bass.ds(st - 2, 1)], min_val=0, max_val=E1 - 1)
                    at_least(pe, gt_copied, st - 1)
                    at_least(pe, y_ready, st - 3)
                    for k in range(NF):
                        last = pe.matmul(DOWN[u % 2], GT[u % 2][:, k * P:(k + 1) * P],
                                         W2[:, bass.ds(e * (NF * D) + k * D, D)], start=(k == 0), stop=(k == NF - 1))
                    last.then_inc(down_done, 1)
                if inside(st + 1):
                    turn_x(st + 1, u + 1)

            pe.wait_ge(slots_ready, 2)
            pe.wait_ge(w12_loaded, 32)
            wait_used(pe, ("vb", 0))
            turn_x(0, 0)
            run_slots(pe, pe_step, NS + 2)

        @block.vector
        def _(dve):
            n_seq = 0

            def seq(ins):
                nonlocal n_seq
                n_seq += 1
                ins.then_inc(dve_seq, 1)
                dve.wait_ge(dve_seq, n_seq)

            def layer_norm(b):
                tiles = range(b * TB, (b + 1) * TB)
                for t in tiles:
                    last = dve.bn_stats(STATS[:, t], X[:, t])
                seq(last)
                for t in tiles:
                    last = dve.bn_aggr(MV[:, t], STATS[:, t])
                seq(last)
                r = slice(b * TB, (b + 1) * TB)
                dve.tensor_scalar(VE[:, r], MV[:, r, 1], LN_EPS, None, ALU.add).then_inc(var_ready, 1)

            def normalise(b, layer=0):
                dve.wait_ge(rstd_ready, layer * B + b + 1)
                for t in range(b * TB, (b + 1) * TB):
                    last = dve.tensor_scalar(XN[:, t, 0:D], X[:, t], MV[:, t, 0:1], RSTD[:, t:t + 1], ALU.subtract, ALU.mult)
                last.then_inc(xn_ready, 1)

            def rank_of(v, n):
                shape = [P, NT, n, n]
                mine = v.rearrange("p t (e o) -> p t e o", o=1).to_broadcast(shape)
                other = v.rearrange("p t (o e) -> p t o e", o=1).to_broadcast(shape)
                cmp = CMP[:, 0:NT * n * n].rearrange("p (t a c) -> p t a c", t=NT, a=n)
                eq = EQ[:, 0:NT * n * n].rearrange("p (t a c) -> p t a c", t=NT, a=n)
                low = LOW[:, 0:n, 0:n].rearrange("p (o a) c -> p o a c", o=1).to_broadcast(shape)
                dve.tensor_tensor(cmp, other, mine, ALU.is_gt)
                seq(dve.tensor_tensor(eq, other, mine, ALU.is_equal))
                seq(dve.tensor_tensor(eq, eq, low, ALU.mult))
                seq(dve.tensor_tensor(cmp, cmp, eq, ALU.add))
                seq(dve.tensor_reduce(RANK[:, :, 0:n], cmp, AX.X, ALU.add))

            def route():
                wait_used(dve, ("lg", 0))
                dve.wait_ge(const_ready, 2)
                bias = GB[:].rearrange("p (o e) -> p o e", o=1).to_broadcast([P, NT, E])
                seq(dve.tensor_tensor(SFC[:], SFC[:], bias, ALU.add))
                seq(dve.tensor_tensor(GS[:], SFC[:, :, 0:E:2], SFC[:, :, 1:E:2], ALU.add))
                rank_of(GS[:], 4)
                seq(dve.tensor_scalar(GS[:], RANK[:, :, 0:4], 2.0, None, ALU.is_lt))
                seq(dve.tensor_tensor(MASKED[:].rearrange("p t (g k) -> p t g k", k=2),
                                      SFC[:].rearrange("p t (g k) -> p t g k", k=2),
                                      GS[:].rearrange("p t (g o) -> p t g o", o=1).to_broadcast([P, NT, 4, 2]),
                                      ALU.mult))
                rank_of(MASKED[:], E)
                seq(dve.scalar_tensor_tensor(out=SFC[:], in0=RANK[:], scalar=2.0, in1=SFC[:],
                                             op0=ALU.is_lt, op1=ALU.mult))
                seq(dve.tensor_reduce(WSUM[:], SFC[:], AX.X, ALU.add))
                seq(dve.tensor_scalar(WSUM[:], WSUM[:], 1e-20, None, ALU.add))
                seq(dve.reciprocal(WSUM[:], WSUM[:]))
                seq(dve.tensor_scalar(WSUM[:], WSUM[:], 2.5, None, ALU.mult))
                seq(dve.tensor_tensor(SFC[:], SFC[:], WSUM[:].rearrange("p (t o) -> p t o", o=1)
                                      .to_broadcast([P, NT, E]), ALU.mult))
                seq(dve.tensor_copy(WPART[:, :, 0], SFC[:]))
                seq(dve.tensor_tensor(SFC[:], SFC[:], WPART[:, :, 0], ALU.subtract))
                seq(dve.tensor_copy(WPART[:, :, 1], SFC[:]))
                dve.tensor_tensor(WPART[:, :, 2], SFC[:], WPART[:, :, 1], ALU.subtract).then_inc(routed, 1)

            def choose(r):
                lo, hi = ROUTES[r]
                wide = [P, hi - lo, E1]
                col = lambda a: a.rearrange("p (t o) -> p t o", o=1).to_broadcast(wide)
                lg, oh, ex = LG[:, lo:hi], OH[:, lo:hi], EXC[:, lo:hi]
                seq(dve.tensor_reduce(MX[:, lo:hi], lg, AX.X, ALU.max))
                dve.tensor_tensor(ex, lg, col(MX[:, lo:hi]), ALU.subtract).then_inc(logits_centred, 1)
                seq(dve.tensor_tensor(oh, lg, col(MX[:, lo:hi]), ALU.is_equal))
                seq(dve.tensor_tensor(oh, oh, PRI[:].rearrange("p (o e) -> p o e", o=1).to_broadcast(wide), ALU.mult))
                seq(dve.tensor_reduce(MX[:, lo:hi], oh, AX.X, ALU.max))
                seq(dve.tensor_tensor(oh, oh, col(MX[:, lo:hi]), ALU.is_equal))
                for e in range(E1):
                    before = PFX[:, lo - 1, e:e + 1] if lo else 0.0
                    last = dve.tensor_tensor_scan(PFX[:, lo:hi, e], ONES[:, 0:hi - lo], oh[:, :, e], before,
                                                  ALU.mult, ALU.add)
                seq(last)
                dve.tensor_tensor(RUN[:, lo:hi], PFX[:, lo:hi], oh, ALU.subtract).then_inc(choice_ready, 1)
                dve.wait_ge(logits_exped, r + 1)
                seq(dve.tensor_reduce(MX[:, lo:hi], ex, AX.X, ALU.add))
                seq(dve.reciprocal(XN[:, lo:hi, COL_SCORE], MX[:, lo:hi]))

            def positions(r):
                lo, hi = ROUTES[r]
                w = bank(("rk", r))
                wait_made(dve, ("rk", r))
                q = EXC[:, lo:hi]
                ranks = w[:, 0:(hi - lo) * E1].rearrange("p (t e) -> p t e", e=E1)
                seq(dve.tensor_tensor(q, ranks, EBASE[:].rearrange("p (o e) -> p o e", o=1)
                                      .to_broadcast([P, hi - lo, E1]), ALU.add))
                seq(dve.tensor_tensor(q, q, OH[:, lo:hi], ALU.mult))
                seq(dve.tensor_reduce(MX[:, lo:hi], q, AX.X, ALU.add))
                dve.tensor_copy(POS[:, lo:hi], MX[:, lo:hi]).then_inc(pos_ready, 1)

            def slot_table():
                w = bank(("rk", 1))
                seq(dve.tensor_scalar(CNTI[:], w[0:1, 128:128 + E1], float(P - 1), None, ALU.add))
                seq(dve.tensor_scalar(CNTI[:], CNTI[:], P.bit_length() - 1, None, ALU.arith_shift_right))
                seq(dve.tensor_copy(CNTF[:], CNTI[:]))
                seq(dve.tensor_tensor_scan(INCL[:], ONES[0:1, 0:E1], CNTF[:], 0.0, ALU.mult, ALU.add))
                wide = [1, NS, E1]
                le = EQ[0:1, 0:NS * E1].rearrange("p (s e) -> p s e", e=E1)
                tl = CMP[0:1, 0:NS * E1].rearrange("p (s e) -> p s e", e=E1)
                seq(dve.tensor_tensor(le, INCL[:].rearrange("p (o e) -> p o e", o=1).to_broadcast(wide),
                                      SLOTI[:].rearrange("p (s o) -> p s o", o=1).to_broadcast(wide), ALU.is_le))
                dve.tensor_tensor(tl, le, CNTF[:].rearrange("p (o e) -> p o e", o=1).to_broadcast(wide), ALU.mult)
                seq(dve.tensor_reduce(STAB[:, 0], le, AX.X, ALU.add))
                seq(dve.tensor_reduce(STAB[:, 1], tl, AX.X, ALU.add))
                seq(dve.tensor_tensor(STAB[:, 2], SLOTI[:], STAB[:, 1], ALU.subtract))
                seq(dve.tensor_scalar(STAB[:, 2], STAB[:, 2], float(P), None, ALU.mult))
                dve.tensor_scalar(SEXP[:], STAB[:, 0], float(E1 - 1), None, ALU.min).then_inc(slots_ready, 1)
                dve.scalar_tensor_tensor(out=SBASE[:], in0=STAB[:, 0], scalar=float(CAP), in1=STAB[:, 2],
                                         op0=ALU.mult, op1=ALU.add).then_inc(slots_ready, 1)

            def head_attention():
                d = DS[:].rearrange("p (b i) h -> p b (i h)", b=B)
                seq(dve.tensor_reduce(SMX[:], d.rearrange("p b x -> p x b"), AX.X, ALU.max))
                wide = [P, B, TB * H]
                m = SMX[:].rearrange("p (o x) -> p o x", o=1).to_broadcast(wide)
                dve.tensor_tensor(d, d, m, ALU.subtract).then_inc(diag_centred, 1)
                dve.wait_ge(diag_exped, 1)
                seq(dve.tensor_reduce(SMX[:], d.rearrange("p b x -> p x b"), AX.X, ALU.add))
                seq(dve.reciprocal(SMX[:], SMX[:]))
                seq(dve.tensor_tensor(d, d, m, ALU.mult))
                wait_used(dve, ("vb", 0))
                for b in range(B):
                    shape = [P, TB, H, HD]
                    probs = DS[:, b * TB:(b + 1) * TB].rearrange("p i (h o) -> p i h o", o=1).to_broadcast(shape)
                    val = VBC[:, b].rearrange("p (o h e) -> p o h e", o=1, h=H).to_broadcast(shape)
                    seq(dve.tensor_tensor(ATT[:].rearrange("p (i h e) -> p i h e", i=TB, h=H), probs, val, ALU.mult))
                    x = X[:, b * TB:(b + 1) * TB].rearrange("p i d -> p (i d)")
                    seq(dve.tensor_tensor(x, x, ATT[:], ALU.add))

            dve.memset(YT[:], 0.0).then_inc(yt_cleared, 1)
            for b in range(B):
                dve.wait_ge(x_loaded[b], 16)
                layer_norm(b)
                if b >= 1:
                    normalise(b - 1)
            normalise(B - 1)
            dve.wait_ge(small_w_loaded, 16 * 5)
            seq(dve.tensor_tensor(WGSQ[:], WGN[:], WGN[:], ALU.mult))
            dve.tensor_reduce(WGNORM[:], WGSQ[:], AX.X, ALU.add).then_inc(sumsq_ready, 1)

            for kind, n in plan:
                item = (kind, n)
                if kind == "cw":
                    wait_made(dve, item)
                    w = bank(item)
                    dve.tensor_copy(WGNT[:], w[0:GATE, 3 * HD:3 * HD + E1])
                    seq(dve.tensor_copy(REP3[:], w[:, 0:3 * HD]))
                    for k, bd in enumerate((BDQ, BDK, BDV)):
                        rep = REP3[:, k * HD:(k + 1) * HD].rearrange("p (o e) -> p o e", o=1).to_broadcast([P, H, HD])
                        ins = dve.tensor_tensor(bd[:].rearrange("p (h e) -> p h e", h=H),
                                                BDMASK[:].rearrange("p (h e) -> p h e", h=H), rep, ALU.mult)
                    used(ins, item)
                if kind == "cm":
                    wait_made(dve, item)
                    used(dve.tensor_copy(BDR[:], bank(item)[:, 0:P + E1]), item)
                if kind == "x2":
                    normalise(n, 1)
                if kind == "d":
                    wait_made(dve, item)
                    t = slice(2 * n, 2 * n + 2)
                    v = bank(item)[:, 0:2 * (P + E1)].rearrange("p (t c) -> p t c", t=2)
                    pr = REST[:, 0:2 * D].rearrange("p (t d) -> p t d", t=2)
                    dve.tensor_copy(LG[:, t], v[:, :, P:])
                    used(dve.tensor_tensor(pr, v[:, :, 0:P], XN[:, t, 0:D], ALU.mult), item)
                    wait_used(dve, item)
                    seq(dve.tensor_reduce(DS[:, t], pr.rearrange("p t (h e) -> p t h e", h=H), AX.X, ALU.add))
                if kind == "ra":
                    choose(n)
                if kind == "rk":
                    positions(n)
                    if n == 1:
                        slot_table()
                    used(dve.tensor_copy(JUNK[:], MX[:, 0:1]), item)
                if kind == "vb":
                    wait_used(dve, ("x2", B - 1))
                    for b in range(B):
                        ins = dve.tensor_scalar(BDVS[:, b], BDV[:], XS[:, b:b + 1], None, ALU.mult)
                    ins.then_inc(bdvs_ready, 1)
                if kind in "qk":
                    s = blk_of(kind, n)[3]
                    dve.wait_ge(first_part, s + 1)
                    part = PARTS[:, s % 3]
                    ins = dve.tensor_tensor(REST[:], bank(item)[:], part[:, 0], ALU.subtract)
                    used(ins, item)
                    wait_used(dve, item)
                    seq(dve.tensor_copy(part[:, 1], REST[:]))
                    dve.tensor_tensor(part[:, 2], REST[:], part[:, 1], ALU.subtract).then_inc(parts_ready, 1)
                    dve.wait_ge(parts_ready, s + 1)
                if kind == "lg":
                    dve.wait_ge(norm_ready, 1)
                    seq(dve.tensor_scalar(WGNORM[:], WGNORM[:], 1e-4, None, ALU.max))
                    seq(dve.reciprocal(WGNORM[:], WGNORM[:]))
                    dve.tensor_scalar(WGN[:], WGN[:], WGNORM[:, 0:1], None, ALU.mult).then_inc(wgn_ready, 1)
                    route()
                if kind == "g":
                    dve.wait_ge(sig_ready, n + 1)
                    used(dve.tensor_tensor(G[:, n % 2], SG[:, n % 2], bank(item)[:], ALU.mult), item)
                if kind == "u":
                    b, j = divmod(n, NJ)
                    wait_made(dve, item)
                    wait_used(dve, ("g", n))
                    if b >= 2 and j == 0:
                        wait_made(dve, ("o", b - 2))
                    used(dve.tensor_tensor(HT[:, b % 2, j], G[:, n % 2], bank(item)[:], ALU.mult), item)
                if kind == "wt":
                    wait_made(dve, item)
                    if n >= 1:
                        wait_made(dve, ("w", (NJ - 1) * n - 1))
                    used(dve.tensor_copy(WTS[:], bank(item)[0:3 * E, 0:L // 2].bitcast(BF16)), item)
                if kind == "w":
                    b, j = divmod(n, NJ - 1)
                    wait_made(dve, item)
                    wait_used(dve, ("u", NJ * b + j))
                    used(dve.tensor_tensor(HT[:, b % 2, j], HT[:, b % 2, j], bank(item)[:], ALU.mult), item)
                if kind == "av" and n % TB == TB - 1:
                    m = n // TB
                    b, hg = divmod(m, 4)
                    dve.wait_ge(av_done, n + 1)
                    if b >= 1 and hg == 0:
                        wait_made(dve, ("n", 2 * (b - 1) + 1))
                    dve.tensor_copy(YS[:, hg], YT[:]).then_inc(yt_saved, 1)
                if kind == "n":
                    b = n // 2
                    wait_made(dve, item)
                    if b >= 1 and n % 2 == 0:
                        wait_used(dve, ("at", b - 1))
                    for k in range(2):
                        i = 2 * (n % 2) + k
                        v = bank(item)[:, k * 144:(k + 1) * 144].rearrange("p (g c) -> p g c", g=4)
                        seq(dve.tensor_scalar(DEN[:].rearrange("p (g h) -> p g h", g=4), v[:, :, 32:36],
                                              2 * ATTN_EPS, CNT[:, i:i + 1], ALU.add, ALU.add))
                        seq(dve.reciprocal(RDEN[:], DEN[:]))
                        o = AO[:, i].rearrange("p (g h e) -> p g h e", g=4, h=4)
                        r = RDEN[:].rearrange("p (g h o) -> p g h o", g=4, o=1).to_broadcast([P, 4, 4, HD])
                        ins = dve.tensor_tensor(o, v[:, :, 0:32].rearrange("p g (h e) -> p g h e", h=4), r, ALU.mult)
                    used(ins, item)
                if kind == "o":
                    wait_made(dve, item)
                    x = X[:, n * TB:(n + 1) * TB].rearrange("p i d -> p (i d)")
                    ins = dve.tensor_tensor(x, x, bank(item)[:], ALU.add)
                    used(ins, item)
                    wait_used(dve, item)
                    layer_norm(n)

            head_attention()

            def dve_step(st, u):
                if inside(st):
                    e = dve.value_load(SEXP[0:1, bass.ds(st, 1)], min_val=0, max_val=E1 - 1)
                    at_least(dve, up_done, st + 1)
                    at_least(dve, gelu_done, st - 1)
                    dve.tensor_tensor(HB[u % 2], SC[:, u % 2, :], B1[:, bass.ds(e * F1, F1)],
                                      ALU.add).then_inc(biased, 1)
                if inside(st - 1):
                    v = (u + 1) % 2
                    at_least(dve, g_turned, st)
                    at_least(dve, down_done, st - 2)
                    dve.tensor_copy(GT[v], SC[:, 2 + v, :]).then_inc(gt_copied, 1)
                if inside(st - 2):
                    e = dve.value_load(SEXP[0:1, bass.ds(st - 2, 1)], min_val=0, max_val=E1 - 1)
                    at_least(dve, down_done, st - 1)
                    at_least(dve, y_scattered[u % 2], 8 * st - (8 * (u % 2) + 16))
                    ins = dve.tensor_tensor(YO[u % 2], DOWN[u % 2], B2[:, bass.ds(e * D, D)], ALU.add)
                    ins.then_inc(y_summed, 1)
                    dve.wait_ge(y_summed, st - 1)
                    dve.tensor_scalar(YO[u % 2], YO[u % 2], SCORE[(u - 2) % U][:], None,
                                      ALU.mult).then_inc(y_ready, 1)
                if inside(st):
                    at_least(dve, xs_loaded[u], loaded(st, u))
                    dve.tensor_copy(SCORE[u][:], XSL[u][:, COL_SCORE:COL_SCORE + 1])
                    dve.tensor_tensor(ROW[u][:], XSL[u][:, COL_ID:COL_ID + 1], PADROW[:, bass.ds(st, 1)],
                                      ALU.min).then_inc(ids_kept, 1)

            dve.wait_ge(b12_loaded, 32)
            run_slots(dve, dve_step, NS + 2)
            for b in range(B):
                dve.wait_ge(y_loaded[b], 16)
                x = X[:, b * TB:(b + 1) * TB]
                dve.tensor_tensor(x, x, YG[:, b * TB:(b + 1) * TB], ALU.add).then_inc(out_ready, 1)


_TURNED = {"L0_attn_Wq", "L0_attn_Wk", "L0_attn_Wv", "L0_attn_Wo", "L1_attn_Wv", "L1_ffn_w_red"}
_INS = ["L0_attn_hidden_states", "L0_attn_Wq", "L0_attn_Wk", "L0_attn_Wv", "L0_attn_Wo", "L0_ffn_gate_w",
        "L0_ffn_gate_bias", "L0_ffn_w_gate", "L0_ffn_w_up", "L0_ffn_w_down", "L0_ffn_sw_gate", "L0_ffn_sw_up",
        "L0_ffn_sw_down", "L1_attn_Wq", "L1_attn_Wk", "L1_attn_Wv", "L1_ffn_w_red", "L1_ffn_wg", "L1_ffn_w1",
        "L1_ffn_b1", "L1_ffn_w2", "L1_ffn_b2"]
_OUTS = [((B, L, D), "float32")]


def kernel(**inputs):
    import numpy as _np
    import concourse.bacc as _bacc
    from concourse import mybir as _mybir
    from concourse.bass_utils import run_bass_kernel_spmd as _run

    nc = _bacc.Bacc("TRN2", target_bir_lowering=False, num_devices=1)
    arrays, args = {}, []
    for name in _INS:
        a = _np.asarray(inputs[name])
        a = _np.ascontiguousarray(a.T if name in _TURNED else a)
        arrays[f"in_{name}_dram"] = a
        args.append(nc.dram_tensor(f"in_{name}_dram", a.shape, _mybir.dt.from_np(a.dtype), kind="ExternalInput").ap())
    for i, (shape, dtype) in enumerate(_OUTS):
        dt = _mybir.dt.from_np(_np.dtype(dtype))
        args.append(nc.dram_tensor(f"out_{i}_dram", shape, dt, kind="ExternalOutput").ap())
    two_layers(nc, *args)
    r = _run(nc, [arrays], core_ids=[0])
    got = tuple(r.results[0][f"out_{i}_dram"] for i in range(len(_OUTS)))
    return got[0]
```

```python
import concourse.bass as bass
from concourse import mybir
from contextlib import ExitStack

F32 = mybir.dt.float32
BF16 = mybir.dt.bfloat16
I32 = mybir.dt.int32
U32 = mybir.dt.uint32
ALU = mybir.AluOpType
ACT = mybir.ActivationFunctionType
AX = mybir.AxisListType

P = 128
B, L, D = 4, 512, 128
TB = L // P
NT = B * TB
T = B * L
H = 16
FEAT = 16
HD = D // H
E = 8
EI = 64
NJ = E * EI // P + 1
F1 = 512
NF = F1 // P
E1 = 8
GATE = 16
CAP = T
U = 4
NS = T // P + E1 - 1
XROWS = E1 * CAP + (E1 - 1) * P
YROWS = T + NS * P
NO_TOKEN = 1.0e6
XW = D + 2
COL_ID = D
COL_SCORE = D + 1
ROUTES = ((0, 3 * TB), (3 * TB, NT))
LN_EPS = 1e-5
ATTN_EPS = 1e-12
SPLIT_Q = (0, 0, 1, 1, 0, 2, 1, 2)
SPLIT_K = (0, 1, 0, 1, 2, 0, 2, 1)
NC = len(SPLIT_Q)
VW = HD + 1
QUAD = 32
A_SLOTS = 3
AV_LAG = 2
SLOT_SCORE = 2


KEY_ORDER = (0, 3, 1, 2)
COST = {"q": 1, "k": 1, "v": 1, "g": 1, "u": 1, "wt": 0.1, "w": 0.3, "n": 1, "at": 0.1, "o": 1.2, "oa": 0.3,
        "x2": 0.3, "lx": 0.4, "d": 1, "cw": 0.4, "cm": 0.5, "ra": 0, "l2": 0, "rk": 0.5, "rt": 0}


def groups():
    return [(b, hg, i) for b in range(B) for hg in range(H // 4) for i in KEY_ORDER]


def project(b):
    return [(k, 2 * b + blk) for blk in range(2) for k in "qk"]


def expert_layer(b):
    return [(k, NJ * b + j) for j in range(NJ) for k in "gu"]


def weigh(b):
    return [("wt", b)] + [("w", (NJ - 1) * b + j) for j in range(NJ - 1)]


def finish(b):
    n, at, o, oa = ([(k, TB * b + i) for i in range(TB)] for k in ("n", "at", "o", "oa"))
    return n + [o[0], at[0], o[1], oa[0], at[1], o[2], oa[1], at[2], o[3], oa[2], at[3], oa[3]]


def turn(b):
    return [("x2", b), ("lx", b), ("d", b)]


def plan_work():
    out = [("ls", 0), ("ln", 0), ("xt", 0)] + project(0)[:2] + [("ls", 1)] + project(0)[2:]
    out += [("v", 0), ("ln", 1), ("xt", 1), ("ls", 2), ("ln", 2), ("xt", 2), ("ls", 3), ("ln", 3), ("xt", 3)]
    out += [("lg", 0)] + project(1) + [("rt", 0)]
    fill = [expert_layer(0) + [("v", 1)] + weigh(0) + [("cw", 0)] + expert_layer(1) + project(2)
            + [("v", 2), ("cm", 0)],
            weigh(1) + finish(0) + [("l2", 0)] + expert_layer(2) + project(3) + [("v", 3)] + turn(0),
            weigh(2) + finish(1) + [("l2", 1)] + expert_layer(3)[:6] + turn(1),
            finish(2) + expert_layer(3)[6:8] + [("l2", 2)] + expert_layer(3)[8:] + weigh(3)[:3] + turn(2)
            + [("ra", 0)] + weigh(3)[3:] + [("rk", 0)]]
    g = groups()
    per = len(g) // B
    for n in range(len(g) + AV_LAG):
        if n < len(g):
            out += [("s", 2 * n), ("s", 2 * n + 1)]
        if n >= AV_LAG:
            out.append(("av", n - AV_LAG))
        b, at = divmod(n, per)
        if b < B and at >= AV_LAG - 1:
            widths = [TB - i for _, _, i in g[b * per + AV_LAG - 1:(b + 1) * per]]
            share = sum(widths[:at - AV_LAG + 2]) / sum(widths)
            total, spent = sum(COST[k] for k, _ in fill[b]), 0.0
            for item in fill[b]:
                spent += COST[item[0]]
                if spent <= share * total + 1e-6 and item not in out:
                    out.append(item)
    assert set(out) >= {item for items in fill for item in items}
    out += finish(B - 1) + [("l2", B - 1), ("x2", B - 1), ("lx", B - 1), ("ra", 1), ("rk", 1), ("d", B - 1), ("vb", 0)]
    return out


def two_layers(nc, x_in, wq_t, wk_t, wv_t, wo_t, gate_w, gate_bias, w_gate, w_up, w_down, sw_gate, sw_up,
               sw_down, head_wq, head_wk, head_wv_t, w_red_t, wg, w1, b1, w2, b2, out):
    plan = plan_work()
    RING_KINDS = ("xt", "q", "k", "v", "lg", "g", "u", "wt", "w", "n", "at", "o",
                  "cw", "cm", "x2", "lx", "d", "rk", "vb")
    place = {item: k for k, item in enumerate(it for it in plan if it[0] in RING_KINDS)}
    RING = 3

    with ExitStack() as ctx:
        def sb(name, shape, dt=F32):
            return ctx.enter_context(nc.sbuf_tensor(name, shape, dt))

        def ps(name, shape):
            return ctx.enter_context(nc.psum_tensor(name, shape, F32))

        def sem(name):
            return ctx.enter_context(nc.semaphore(name))

        X = sb("X", [P, NT, D])
        XN = sb("XN", [P, NT, XW])
        XNT = sb("XNT", [P, T])
        WQ = sb("WQ", [P, H * FEAT])
        WK = sb("WK", [P, H * FEAT])
        WV = sb("WV", [P, D])
        WO = sb("WO", [P, D])
        GW = sb("GW", [P, E])
        GB = sb("GB", [P, E])
        WG = sb("WG", [P, NJ * P])
        WU = sb("WU", [P, NJ * P])
        WD = sb("WD", [P, NJ, D])
        IDF = sb("IDF", [P, P])
        IDB = sb("IDB", [P, P], BF16)
        TRI = sb("TRI", [P, P])
        ONES = sb("ONES", [P, P])
        SEL = sb("SEL", [P, 36])
        SELW = sb("SELW", [3 * E, NJ - 1, P], BF16)
        LOW = sb("LOW", [P, E, E])
        CNT = sb("CNT", [P, TB])
        NHALF = sb("NHALF", [P, NT])
        NROOT = sb("NROOT", [E, 1])
        STATS = sb("STATS", [P, NT, 6])
        MV = sb("MV", [P, NT, 2])
        VE = sb("VE", [P, NT])
        RSTD = sb("RSTD", [P, NT])
        PARTS = sb("PARTS", [P, 3, 3, L], BF16)
        REST = sb("REST", [P, L])
        STK = [sb(f"STK{n}", [P, 2, H, L], BF16) for n in range(2)]
        VH = sb("VH", [P, 3, TB, H, VW])
        VP = sb("VP", [P, 2, 2, H, HD])
        A = sb("A", [P, A_SLOTS, 4, L])
        YS = sb("YS", [P, 4, L])
        DEN = sb("DEN", [P, H])
        RDEN = sb("RDEN", [P, H])
        AO = sb("AO", [P, TB, D])
        AOT = sb("AOT", [P, TB, P])
        SG = sb("SG", [P, 2, L])
        G = sb("G", [P, 2, L])
        HT = sb("HT", [P, 2, NJ, L])
        WTS = sb("WTS", [3 * E, L], BF16)
        SFC = sb("SFC", [P, NT, E])
        GS = sb("GS", [P, NT, 4])
        CMP = YS[:, 0:2, :].rearrange("p a n -> p (a n)")
        EQ = YS[:, 2:4, :].rearrange("p a n -> p (a n)")
        RANK = sb("RANK", [P, NT, E])
        MASKED = sb("MASKED", [P, NT, E])
        WSUM = sb("WSUM", [P, NT])
        WPART = sb("WPART", [P, NT, 3, E], BF16)

        W8 = sb("W8", [HD, 3 * HD])
        WGN = sb("WGN", [E1, GATE])
        WGSQ = sb("WGSQ", [E1, GATE])
        WGNORM = sb("WGNORM", [E1, 1])
        REDT = sb("REDT", [GATE, P])
        WGNT = sb("WGNT", [GATE, E1])
        REPL = sb("REPL", [HD, P])
        BDMASK = sb("BDMASK", [P, P])
        REP3 = sb("REP3", [P, 3 * HD])
        BDQ = sb("BDQ", [P, P])
        BDK = sb("BDK", [P, P])
        BDV = sb("BDV", [P, P])
        BDR = sb("BDR", [P, P + E1])
        INIT = sb("INIT", [P, XW])
        XS = sb("XS", [P, B])
        PADROW = sb("PADROW", [P, NS])
        ROW = [sb(f"ROW{n}", [P, 1], U32) for n in range(U)]
        SCORE = [sb(f"SCORE{n}", [P, 1]) for n in range(U)]
        DS = sb("DS", [P, NT, H])
        LG = sb("LG", [P, NT, E1])
        MX = sb("MX", [P, NT])
        PRI = sb("PRI", [P, E1])
        OH = sb("OH", [P, NT, E1])
        PFX = sb("PFX", [P, NT, E1])
        EXC = sb("EXC", [P, NT, E1])
        EBASE = sb("EBASE", [P, E1])
        POS = sb("POS", [P, NT], U32)
        SLOTI = sb("SLOTI", [1, NS])
        CNTI = sb("CNTI", [1, E1], I32)
        CNTF = sb("CNTF", [1, E1])
        INCL = sb("INCL", [1, E1])
        STAB = sb("STAB", [1, 4, NS])
        SEXP = sb("SEXP", [1, NS], I32)
        SBASE = sb("SBASE", [1, NS], I32)
        JUNK = sb("JUNK", [P, 1])
        SMX = sb("SMX", [P, TB * H])
        W1 = STK[0][:, 0].rearrange("p h t -> p (h t)").bitcast(F32)
        W2 = STK[0][:, 1].rearrange("p h t -> p (h t)").bitcast(F32)
        B1 = STK[1][:, 0].rearrange("p h t -> p (h t)").bitcast(F32)
        B2 = STK[1][:, 1, 0:4].rearrange("p h t -> p (h t)").bitcast(F32)
        HB = [A[:, 0, n] for n in range(2)]
        GE = [A[:, 0, 2 + n] for n in range(2)]
        GT = [A[:, 1, n] for n in range(2)]
        XTS = [A[:, 1, 2, n * P:(n + 1) * P] for n in range(2)]
        YO = [A[:, 1, 3, n * P:(n + 1) * P] for n in range(2)]
        XSL = [A[:, 2, n, 0:XW] for n in range(U)]
        YG = HT[:, 0, 0:4].rearrange("p j t -> p (j t)").rearrange("p (t d) -> p t d", d=D)
        RUN = MASKED
        BDVS = sb("BDVS", [P, B, D])
        VBC = AO
        ATT = REST

        xs_dram = nc.dram_tensor("xs_dram", [XROWS, XW], F32, kind="Internal").ap()
        y_dram = nc.dram_tensor("y_dram", [YROWS, D], F32, kind="Internal").ap()
        parts_dram = nc.dram_tensor("parts_dram", [B, 2, 3, H, FEAT, L], BF16, kind="Internal").ap()

        SC = ps("SC", [P, 4, L])
        YT = ps("YT", [P, L])
        WB = [ps(f"WB{r}", [P, L]) for r in range(RING)]

        DOWN = [WB[2][:, 0:P], YT[:, 0:P]]

        x_loaded = [sem(f"x_loaded{b}") for b in range(B)]
        qkv_w_loaded = sem("qkv_w_loaded")
        ffn_w_loaded = sem("ffn_w_loaded")
        const_ready = sem("const_ready")
        ones_ready = sem("ones_ready")
        var_ready = sem("var_ready")
        rstd_ready = sem("rstd_ready")
        xn_ready = sem("xn_ready")
        work_ready = [sem(f"work_ready{r}") for r in range(RING)]
        work_used = [sem(f"work_used{r}") for r in range(RING)]
        first_part = sem("first_part")
        sig_ready = sem("sig_ready")
        parts_ready = sem("parts_ready")
        parts_saved = [sem(f"parts_saved{n}") for n in range(3)]
        stack_loaded = [[sem(f"stack_loaded{n}_{blk}") for blk in range(2)] for n in range(2)]
        score_ready = [sem(f"score_ready{n}") for n in range(2)]
        squared = sem("squared")
        masked = sem("masked")
        av_done = sem("av_done")
        yt_cleared = sem("yt_cleared")
        yt_saved = sem("yt_saved")
        v_prefix = sem("v_prefix")
        routed = sem("routed")
        small_w_loaded = sem("small_w_loaded")
        w12_loaded = sem("w12_loaded")
        b12_loaded = sem("b12_loaded")
        consts1 = sem("consts1")
        sumsq_ready = sem("sumsq_ready")
        norm_ready = sem("norm_ready")
        wgn_ready = sem("wgn_ready")
        init_ready = sem("init_ready")
        xs_cleared = sem("xs_cleared")
        logits_centred = sem("logits_centred")
        logits_exped = sem("logits_exped")
        choice_ready = sem("choice_ready")
        pos_ready = sem("pos_ready")
        xs_scattered = sem("xs_scattered")
        slots_ready = sem("slots_ready")
        bdvs_ready = sem("bdvs_ready")
        diag_centred = sem("diag_centred")
        diag_exped = sem("diag_exped")
        xs_loaded = [sem(f"xs_loaded{n}") for n in range(U)]
        ids_kept = sem("ids_kept")
        x_turned = sem("x_turned")
        xt_copied = sem("xt_copied")
        up_done = sem("up_done")
        biased = sem("biased")
        gelu_done = sem("gelu_done")
        g_turned = sem("g_turned")
        gt_copied = sem("gt_copied")
        down_done = sem("down_done")
        y_summed = sem("y_summed")
        y_ready = sem("y_ready")
        y_scatter_begun = sem("y_scatter_begun")
        y_scattered = [sem(f"y_scattered{n}") for n in range(2)]
        y_loaded = [sem(f"y_loaded{b}") for b in range(B)]
        out_ready = sem("out_ready")
        saved = sem("saved")
        dve_seq = sem("dve_seq")
        pool_seq = sem("pool_seq")

        block = ctx.enter_context(nc.Block())

        def bank(item):
            return WB[place[item] % RING]

        def wait_bank(eng, item):
            k = place[item]
            if k >= RING:
                eng.wait_ge(work_used[k % RING], k // RING)

        def wait_made(eng, item):
            k = place[item]
            eng.wait_ge(work_ready[k % RING], k // RING + 1)

        def made(ins, item):
            ins.then_inc(work_ready[place[item] % RING], 1)

        def wait_used(eng, item):
            k = place[item]
            eng.wait_ge(work_used[k % RING], k // RING + 1)

        def used(ins, item):
            ins.then_inc(work_used[place[item] % RING], 1)

        def blk_of(kind, n):
            b, blk = divmod(n, 2)
            return b, int(kind == "k"), blk, 4 * b + 2 * blk + int(kind == "k")

        def inside(s):
            return not isinstance(s, int) or 0 <= s < NS

        def at_least(eng, semaphore, v):
            if not isinstance(v, int) or v > 0:
                eng.wait_ge(semaphore, v)

        def loaded(s, u):
            return 16 // U * s + (16 - 16 // U * (u % U))

        def run_slots(eng, step, end):
            full = (NS - 1) // U
            for s in range(U):
                step(s, s)
            with eng.Fori(1, full) as m:
                for u in range(U):
                    step(m * U + u, u)
            for s in range(full * U, end):
                step(s, s % U)

        xt_in = x_in.rearrange("b (i p) d -> b p i d", p=P)
        xt_out = out.rearrange("b (i p) d -> b p i d", p=P)

        @block.sync
        def _(sp):
            def load_x(b):
                sp.dma_start(X[:, b * TB:(b + 1) * TB, :], xt_in[b]).then_inc(x_loaded[b], 16)

            load_x(0)
            sp.dma_start(WQ[:], wq_t).then_inc(qkv_w_loaded, 16)
            sp.dma_start(WK[:], wk_t).then_inc(qkv_w_loaded, 16)
            sp.dma_start(WV[:], wv_t).then_inc(qkv_w_loaded, 16)
            for b in range(1, B):
                load_x(b)
            nr = (NJ - 1) * P
            sp.dma_start(GW[:], gate_w).then_inc(ffn_w_loaded, 16)
            sp.dma_start(GB[:], gate_bias.rearrange("(a e) -> a e", a=1).to_broadcast([P, E])).then_inc(ffn_w_loaded, 16)
            sp.dma_start(WG[:, 0:nr].rearrange("h (e i) -> h e i", e=E),
                         w_gate.rearrange("e h i -> h e i")).then_inc(ffn_w_loaded, 16)
            sp.dma_start(WG[:, nr:], sw_gate).then_inc(ffn_w_loaded, 16)
            sp.dma_start(WU[:, 0:nr].rearrange("h (e i) -> h e i", e=E),
                         w_up.rearrange("e h i -> h e i")).then_inc(ffn_w_loaded, 16)
            sp.dma_start(WU[:, nr:], sw_up).then_inc(ffn_w_loaded, 16)
            sp.dma_start(WD[:, 0:NJ - 1], w_down.rearrange("(j e) i h -> (e i) j h", e=2)).then_inc(ffn_w_loaded, 16)
            sp.dma_start(WD[:, NJ - 1], sw_down).then_inc(ffn_w_loaded, 16)
            sp.dma_start(WO[:], wo_t).then_inc(ffn_w_loaded, 16)
            sp.dma_start(W8[:, 0:HD], head_wq).then_inc(small_w_loaded, 16)
            sp.dma_start(W8[:, HD:2 * HD], head_wk).then_inc(small_w_loaded, 16)
            sp.dma_start(W8[:, 2 * HD:], head_wv_t).then_inc(small_w_loaded, 16)
            sp.dma_start(REDT[:], w_red_t).then_inc(small_w_loaded, 16)
            sp.dma_start(WGN[:], wg).then_inc(small_w_loaded, 16)

            def save_parts(b, blk):
                for qk in range(2):
                    n = 4 * b + 2 * blk + qk
                    sp.wait_ge(parts_ready, n + 1)
                    dst = parts_dram[b, qk, :, 8 * blk:8 * blk + 8].rearrange("c h d t -> (h d) c t")
                    sp.dma_start(dst, PARTS[:, n % 3]).then_inc(parts_saved[n % 3], 16)

            def load_stack(b, blk):
                for n in range(4 * b + 2 * blk, 4 * b + 2 * blk + 2):
                    sp.wait_ge(parts_saved[n % 3], 16 * (n // 3 + 1))
                if b >= 2:
                    for half in range(2):
                        sp.wait_ge(score_ready[half], 4 * TB * (b - 1))
                hs = slice(8 * blk, 8 * blk + 8)
                for c in range(NC):
                    for qk, parts in ((0, SPLIT_Q), (1, SPLIT_K)):
                        src = parts_dram[b, qk, parts[c], hs].rearrange("h d t -> d h t")
                        sp.dma_start(STK[b % 2][FEAT * c:FEAT * (c + 1), qk, hs], src)\
                            .then_inc(stack_loaded[b % 2][blk], 16)

            for b in range(B):
                save_parts(b, 0)
                if b == 0:
                    load_stack(b, 0)
                save_parts(b, 1)
                if b == 2:
                    sp.wait_ge(init_ready, 1)
                    rows = xs_dram.rearrange("(j p) c -> p j c", p=P)
                    sp.dma_start(rows, INIT[:].rearrange("p (o c) -> p o c", o=1)
                                 .to_broadcast([P, XROWS // P, XW])).then_inc(xs_cleared, 16)
                if b > 0:
                    load_stack(b, 0)
                load_stack(b, 1)
            sp.wait_ge(score_ready[0], 4 * TB * 3)
            sp.wait_ge(score_ready[1], 4 * TB * 3)
            sp.dma_start(W1.rearrange("p (e f) -> p e f", e=E1), w1.rearrange("e d f -> d e f")).then_inc(w12_loaded, 16)
            sp.dma_start(W2.rearrange("p (e k d) -> p e k d", e=E1, k=NF),
                         w2.rearrange("e (k p) d -> p e k d", p=P)).then_inc(w12_loaded, 16)
            sp.wait_ge(score_ready[0], 4 * TB * 4)
            sp.wait_ge(score_ready[1], 4 * TB * 4)
            sp.dma_start(B1, b1.rearrange("(o e) f -> o (e f)", o=1).to_broadcast([P, E1 * F1])).then_inc(b12_loaded, 16)
            sp.dma_start(B2, b2.rearrange("(o e) f -> o (e f)", o=1).to_broadcast([P, E1 * D])).then_inc(b12_loaded, 16)
            sp.wait_ge(slots_ready, 2)
            sp.wait_ge(xs_scattered, 16 * NT)

            def load_slot(s, u):
                at_least(sp, x_turned, s - U + 1)
                at_least(sp, ids_kept, s - U + 1)
                row = sp.value_load(SBASE[0:1, bass.ds(s, 1)], min_val=0, max_val=XROWS - P)
                sp.dma_start(XSL[u], xs_dram[bass.ds(row, P), :]).then_inc(xs_loaded[u], 16)

            run_slots(sp, load_slot, NS)
            for n in range(2):
                sp.wait_ge(y_scattered[n], 16 * ((NS + 1 - n) // 2))
            y_tok = y_dram[0:T].rearrange("(b i p) d -> b p i d", b=B, p=P)
            for b in range(B):
                sp.dma_start(YG[:, b * TB:(b + 1) * TB], y_tok[b]).then_inc(y_loaded[b], 16)
            for b in range(B):
                sp.wait_ge(out_ready, b + 1)
                sp.dma_start(xt_out[b], X[:, b * TB:(b + 1) * TB, :]).then_inc(saved, 16)
            sp.wait_ge(saved, 16 * B)

        @block.gpsimd
        def _(pool):
            n_seq = 0

            def seq(ins):
                nonlocal n_seq
                n_seq += 1
                ins.then_inc(pool_seq, 1)
                pool.wait_ge(pool_seq, n_seq)

            seq(pool.memset(NHALF[:], -0.5))
            seq(pool.memset(IDF[:], 0.0))
            pool.affine_select(out=IDF[:], in_=IDF[:], pattern=[[-1, P]], compare_op=ALU.not_equal,
                               fill=1.0, base=0, channel_multiplier=1).then_inc(const_ready, 1)
            pool.memset(VH[:, :, :, :, HD:HD + 1], 1.0).then_inc(ones_ready, 1)

            def rstd(m):
                pool.wait_ge(var_ready, m + 1)
                r = slice(m % B * TB, (m % B + 1) * TB)
                pool.tensor_tensor(RSTD[:, r], VE[:, r], NHALF[:, r], ALU.pow).then_inc(rstd_ready, 1)

            def constants0():
                pool.memset(ONES[:], 1.0)
                seq(pool.memset(TRI[:], 1.0))
                seq(pool.affine_select(out=TRI[:], in_=TRI[:], pattern=[[1, P]], compare_op=ALU.is_ge,
                                       fill=0.0, base=0, channel_multiplier=-1))
                seq(pool.memset(IDB[:], 0.0))
                seq(pool.affine_select(out=IDB[:], in_=IDB[:], pattern=[[-1, P]], compare_op=ALU.not_equal,
                                       fill=1.0, base=0, channel_multiplier=1))
                seq(pool.memset(SEL[:], 0.0))
                v = SEL[:, 0:32].rearrange("p (h e) -> p h e", h=4)
                pool.affine_select(out=v, in_=v, pattern=[[-QUAD, 4], [-1, HD]], compare_op=ALU.not_equal,
                                   fill=1.0, base=0, channel_multiplier=1)
                seq(pool.affine_select(out=SEL[:, 32:36], in_=SEL[:, 32:36], pattern=[[-QUAD, 4]],
                                       compare_op=ALU.not_equal, fill=1.0, base=-HD, channel_multiplier=1))
                seq(pool.memset(LOW[:], 1.0))
                seq(pool.affine_select(out=LOW[:], in_=LOW[:], pattern=[[1, E], [-1, E]], compare_op=ALU.is_gt,
                                       fill=0.0, base=0, channel_multiplier=0))
                seq(pool.memset(SELW[:], 0.0))
                v = SELW[:].rearrange("k j (e f) -> k j e f", e=2)
                for c in range(3):
                    seq(pool.affine_select(out=v, in_=v, pattern=[[-2, NJ - 1], [-1, 2], [0, EI]],
                                           compare_op=ALU.not_equal, fill=1.0, base=-E * c, channel_multiplier=1))
                pool.iota(CNT[:], [[P, TB]], base=1, channel_multiplier=1,
                          allow_small_or_imprecise_dtypes=True).then_inc(const_ready, 1)
            def constants1():
                seq(pool.memset(REPL[:], 0.0))
                v = REPL[:].rearrange("p (h e) -> p h e", h=H)
                pool.affine_select(out=v, in_=v, pattern=[[0, H], [-1, HD]], compare_op=ALU.not_equal,
                                   fill=1.0, base=0, channel_multiplier=1)
                seq(pool.memset(BDMASK[:], 1.0))
                v = BDMASK[:].rearrange("p (h e) -> p h e", h=H)
                seq(pool.affine_select(out=v, in_=v, pattern=[[-HD, H], [0, HD]], compare_op=ALU.is_ge,
                                       fill=0.0, base=0, channel_multiplier=1))
                seq(pool.affine_select(out=v, in_=v, pattern=[[HD, H], [0, HD]], compare_op=ALU.is_ge,
                                       fill=0.0, base=HD - 1, channel_multiplier=-1))
                pool.iota(PRI[:], [[-1, E1]], base=E1, channel_multiplier=0, allow_small_or_imprecise_dtypes=True)
                pool.iota(EBASE[:], [[CAP, E1]], base=-1, channel_multiplier=0, allow_small_or_imprecise_dtypes=True)
                seq(pool.iota(SLOTI[:], [[1, NS]], base=0, channel_multiplier=0, allow_small_or_imprecise_dtypes=True))
                pool.iota(PADROW[:], [[P, NS]], base=T, channel_multiplier=1, allow_small_or_imprecise_dtypes=True)
                seq(pool.memset(INIT[:], 0.0))
                pool.memset(INIT[:, COL_ID:COL_ID + 1], NO_TOKEN).then_inc(init_ready, 1)
                seq(pool.iota(XN[:, :, COL_ID:COL_ID + 1], [[P, NT], [1, 1]], base=0, channel_multiplier=1,
                              allow_small_or_imprecise_dtypes=True))
                seq(pool.memset(NROOT[:], 0.5))
                pool.nop().then_inc(consts1, 1)
                pool.wait_ge(sumsq_ready, 1)
                pool.tensor_tensor(WGNORM[:], WGNORM[:], NROOT[:], ALU.pow).then_inc(norm_ready, 1)

            def scatter(r):
                lo, hi = ROUTES[r]
                pool.wait_ge(pos_ready, r + 1)
                if r == 0:
                    pool.wait_ge(xs_cleared, 16)
                for t in range(lo, hi):
                    pool.indirect_dma_start(out=xs_dram[:, :], out_offset=bass.IndirectOffsetOnAxis(ap=POS[:, t:t + 1], axis=0),
                                            in_=XN[:, t], in_offset=None).then_inc(xs_scattered, 16)

            for kind, n in plan:
                if kind == "ls":
                    rstd(n)
                    if n == 0:
                        constants0()
                    if n == 3:
                        constants1()
                if kind == "l2":
                    rstd(B + n)
                if kind == "rk":
                    scatter(n)
                if kind == "s":
                    pool.wait_ge(squared, n + 1)
                    g = n // 2
                    a = A[:, g % A_SLOTS, 2 * (n % 2):2 * (n % 2) + 2, 0:P]
                    pool.affine_select(out=a, in_=a, pattern=[[0, 2], [1, P]], compare_op=ALU.is_ge,
                                       fill=0.0, base=0, channel_multiplier=-1).then_inc(masked, 1)
                if kind == "s" and n % (8 * TB) == 0:
                    b = n // (8 * TB)
                    wait_used(pool, ("v", b))
                    if b >= 2:
                        wait_made(pool, ("n", TB * (b - 2) + TB - 1))
                    vb = VH[:, b % 3, :, :, 0:HD]
                    seq(pool.tensor_tensor(VP[:, b % 2, 0], vb[:, 0], vb[:, 1], ALU.add))
                    pool.tensor_tensor(VP[:, b % 2, 1], VP[:, b % 2, 0], vb[:, 2], ALU.add).then_inc(v_prefix, 1)

            def scatter_y(s, u):
                at_least(pool, y_ready, s + 1)
                pool.sem_inc(y_scatter_begun, 1)
                pool.indirect_dma_start(out=y_dram[:, :],
                                        out_offset=bass.IndirectOffsetOnAxis(ap=ROW[u][:], axis=0),
                                        in_=YO[u % 2], in_offset=None).then_inc(y_scattered[u % 2], 16)

            run_slots(pool, scatter_y, NS)

        @block.scalar
        def _(act):
            for kind, n in plan:
                item = (kind, n)
                if kind == "xt":
                    wait_made(act, item)
                    used(act.copy(XNT[:, n * L:(n + 1) * L], bank(item)[:]), item)
                if kind in "qk":
                    s = blk_of(kind, n)[3]
                    wait_made(act, item)
                    if s >= 3:
                        act.wait_ge(parts_saved[s % 3], 16 * (s // 3))
                    act.copy(PARTS[:, s % 3, 0], bank(item)[:]).then_inc(first_part, 1)
                if kind == "v":
                    wait_made(act, item)
                    act.wait_ge(ones_ready, 1)
                    if n >= 3:
                        wait_made(act, ("n", TB * (n - 3) + TB - 1))
                    used(act.copy(VH[:, n % 3, :, :, 0:HD],
                                  bank(item)[:].rearrange("p (i h e) -> p i h e", i=TB, h=H)), item)
                if kind == "lg":
                    wait_made(act, item)
                    used(act.activation(SFC[:], bank(item)[:, 0:NT * E].rearrange("p (t e) -> p t e", e=E),
                                        ACT.Sigmoid), item)
                if kind == "g":
                    wait_made(act, item)
                    if n >= 2:
                        wait_used(act, ("g", n - 2))
                    act.activation(SG[:, n % 2], bank(item)[:], ACT.Sigmoid).then_inc(sig_ready, 1)
                if kind == "s":
                    g, half = divmod(n, 2)
                    w = L - P * groups()[g][2]
                    act.wait_ge(score_ready[half], g + 1)
                    if g >= A_SLOTS:
                        act.wait_ge(av_done, g - A_SLOTS + 1)
                    act.activation(A[:, g % A_SLOTS, 2 * half:2 * half + 2, 0:w], SC[:, 2 * half:2 * half + 2, 0:w],
                                   ACT.Square, bias=1.0, scale=0.25).then_inc(squared, 1)
                if kind == "at":
                    wait_made(act, item)
                    if n >= TB:
                        wait_made(act, ("o", n - TB))
                    used(act.copy(AOT[:, n % TB], bank(item)[:, 0:P]), item)
                if kind == "x2":
                    wait_made(act, item)
                    used(act.activation(XNT[:, n * L:(n + 1) * L], bank(item)[:], ACT.Identity,
                                        accum_out=XS[:, n:n + 1]), item)
                if kind == "ra":
                    lo, hi = ROUTES[n]
                    act.wait_ge(logits_centred, n + 1)
                    act.activation(EXC[:, lo:hi], EXC[:, lo:hi], ACT.Exp).then_inc(logits_exped, 1)
                if kind == "vb":
                    wait_made(act, item)
                    used(act.copy(VBC[:].rearrange("p b d -> p (b d)"), bank(item)[:]), item)

            act.wait_ge(diag_centred, 1)
            act.activation(DS[:], DS[:], ACT.Exp, scale=D ** -0.5).then_inc(diag_exped, 1)

            def act_step(st, u):
                if inside(st + 1):
                    copy_x(st + 1, u + 1)
                if inside(st - 1):
                    v = (u + 1) % 2
                    at_least(act, g_turned, st)
                    at_least(act, down_done, st - 2)
                    act.copy(GT[v], SC[:, 2 + v, :]).then_inc(gt_copied, 1)
                if inside(st):
                    at_least(act, biased, st + 1)
                    at_least(act, g_turned, st - 1)
                    act.activation(GE[u % 2], HB[u % 2], ACT.Gelu).then_inc(gelu_done, 1)

            def copy_x(s, u):
                at_least(act, x_turned, s + 1)
                at_least(act, up_done, s - 1)
                act.copy(XTS[u % 2], WB[u % 2][:, 0:P]).then_inc(xt_copied, 1)

            act.wait_ge(slots_ready, 2)
            copy_x(0, 0)
            run_slots(act, act_step, NS + 1)

        @block.tensor
        def _(pe):
            for kind, n in plan:
                item = (kind, n)
                if kind in RING_KINDS:
                    wait_bank(pe, item)
                    w = bank(item)
                if kind == "xt":
                    if n == 0:
                        pe.wait_ge(const_ready, 1)
                    pe.wait_ge(xn_ready, n + 1)
                    for i in range(TB):
                        last = pe.transpose(w[:, i * P:(i + 1) * P], XN[:, n * TB + i, 0:D], IDF[:])
                if kind in "qk":
                    b, qk, blk, s = blk_of(kind, n)
                    if s == 0:
                        pe.wait_ge(qkv_w_loaded, 48)
                    wait_used(pe, ("xt", b))
                    last = pe.matmul(w[:], (WQ, WK)[qk][:, blk * P:(blk + 1) * P], XNT[:, b * L:(b + 1) * L],
                                     start=True, stop=True)
                if kind == "v":
                    wait_used(pe, ("xt", n))
                    for i in range(TB):
                        t = n * TB + i
                        last = pe.matmul(w[:, i * P:(i + 1) * P], XNT[:, t * P:(t + 1) * P], WV[:],
                                         start=(i == 0), stop=True, skip_group_check=True)
                if kind == "lg":
                    for b in range(B):
                        wait_used(pe, ("xt", b))
                    for t in range(NT):
                        last = pe.matmul(w[:, t * E:(t + 1) * E], XNT[:, t * P:(t + 1) * P], GW[:],
                                         start=(t == 0), stop=True, skip_group_check=True)
                if kind in "gu":
                    b, j = divmod(n, NJ)
                    if item == ("g", 0):
                        pe.wait_ge(ffn_w_loaded, 144)
                    wait_used(pe, ("xt", b))
                    last = pe.matmul(w[:], (WG if kind == "g" else WU)[:, j * P:(j + 1) * P],
                                     XNT[:, b * L:(b + 1) * L], start=True, stop=True)
                if kind == "wt":
                    if n == 0:
                        pe.wait_ge(routed, 1)
                        pe.wait_ge(const_ready, 2)
                    for i in range(TB):
                        last = pe.transpose(w[0:3 * E, 0:L // 2].bitcast(BF16)[:, i * P:(i + 1) * P],
                                            WPART[:, n * TB + i].rearrange("p c e -> p (c e)"), IDB[:])
                if kind == "w":
                    b, j = divmod(n, NJ - 1)
                    wait_used(pe, ("wt", b))
                    last = pe.matmul(w[:], SELW[:, j], WTS[:], start=True, stop=True)
                if kind == "s":
                    g, half = divmod(n, 2)
                    b, hg, i = groups()[g]
                    if g % (2 * TB) == 0 and half == 0:
                        pe.wait_ge(stack_loaded[b % 2][hg // 2], 16 * 2 * NC * (b // 2 + 1))
                    if g >= 1:
                        pe.wait_ge(squared, 2 * (g - 1) + half + 1)
                    for k in range(2):
                        h = 4 * hg + 2 * half + k
                        last = pe.matmul(SC[:, 2 * half + k, 0:L - P * i], STK[b % 2][:, 1, h, i * P:(i + 1) * P],
                                         STK[b % 2][:, 0, h, i * P:L], start=True, stop=True)
                    last.then_inc(score_ready[half], 1)
                if kind == "av":
                    b, hg, i = groups()[n]
                    pe.wait_ge(masked, 2 * n + 2)
                    if n == 0:
                        pe.wait_ge(yt_cleared, 1)
                    if i == 0 and n > 0:
                        pe.wait_ge(yt_saved, n // TB)
                    for k in range(4):
                        last = pe.matmul(YT[QUAD * k:QUAD * k + VW, i * P:L], VH[:, b % 3, i, 4 * hg + k],
                                         A[:, n % A_SLOTS, k, 0:L - P * i], start=(i == 0), stop=(n % TB == TB - 1),
                                         skip_group_check=True)
                    last.then_inc(av_done, 1)
                if kind == "n":
                    b, i = divmod(n, TB)
                    pe.wait_ge(yt_saved, 4 * (b + 1))
                    pe.wait_ge(v_prefix, b + 1)
                    num = w[:, 0:144].rearrange("p (g c) -> p g c", g=4)[:, :, 0:32]\
                        .rearrange("p g (h e) -> p g h e", h=4)
                    vi = VH[:, b % 3, i, :, 0:HD].rearrange("p (g h) e -> p g h e", g=4)
                    pe.matmul(num, TRI[:], vi, start=True, stop=False, skip_group_check=True)
                    if i >= 1:
                        before = VH[:, b % 3, 0, :, 0:HD] if i == 1 else VP[:, b % 2, i - 2]
                        pe.matmul(num, ONES[:], before.rearrange("p (g h) e -> p g h e", g=4), start=False,
                                  stop=False, skip_group_check=True)
                    for hg in range(4):
                        last = pe.matmul(w[:, hg * 36:hg * 36 + 36], YS[:, hg, i * P:(i + 1) * P], SEL[:],
                                         start=False, stop=True, skip_group_check=True)
                if kind == "at":
                    wait_used(pe, ("n", n))
                    last = pe.transpose(w[:, 0:P], AO[:, n % TB], IDF[:])
                if kind == "o":
                    b, i = divmod(n, TB)
                    wait_used(pe, ("w", (NJ - 1) * b + NJ - 2))
                    wait_used(pe, ("u", NJ * b + NJ - 1))
                    for j in range(NJ):
                        pe.matmul(w[:, 0:P], HT[:, b % 2, j, i * P:(i + 1) * P], WD[:, j], start=(j == 0),
                                  stop=False, skip_group_check=True)
                if kind == "oa":
                    wait_used(pe, ("at", n))
                    made(pe.matmul(bank(("o", n))[:, 0:P], AOT[:, n % TB], WO[:], start=False, stop=True,
                                   skip_group_check=True), ("o", n))
                if kind == "cw":
                    pe.wait_ge(small_w_loaded, 16 * 5)
                    pe.wait_ge(consts1, 1)
                    pe.wait_ge(wgn_ready, 1)
                    pe.matmul(w[:, 0:3 * HD], REPL[:], W8[:], start=True, stop=True)
                    last = pe.transpose(w[0:GATE, 3 * HD:3 * HD + E1], WGN[:], IDF[0:E1, 0:E1])
                if kind == "cm":
                    wait_used(pe, ("cw", 0))
                    pe.matmul(w[:, 0:P], BDQ[:], BDK[:], start=True, stop=True)
                    last = pe.matmul(w[:, P:P + E1], REDT[:], WGNT[:], start=False, stop=True, skip_group_check=True)
                if kind == "x2":
                    pe.wait_ge(xn_ready, B + n + 1)
                    for i in range(TB):
                        last = pe.transpose(w[:, i * P:(i + 1) * P], XN[:, n * TB + i, 0:D], IDF[:])
                if kind == "d":
                    for i in range(TB):
                        t = TB * n + i
                        last = pe.matmul(w[:, i * P:(i + 1) * P], XNT[:, t * P:(t + 1) * P], BDR[:, 0:P],
                                         start=(i == 0), stop=True, skip_group_check=True)
                if kind == "rk":
                    pe.wait_ge(choice_ready, n + 1)
                    lo, hi = ROUTES[n]
                    c = (hi - lo) * E1
                    pe.matmul(w[:, 0:c], TRI[:], OH[:, lo:hi], start=True, stop=False, skip_group_check=True)
                    last = pe.matmul(w[:, 0:c], ONES[:], RUN[:, lo:hi], start=False, stop=True, skip_group_check=True)
                    if hi == NT:
                        last = pe.matmul(w[:, 128:128 + E1], ONES[:], PFX[:, NT - 1], start=False, stop=True,
                                         skip_group_check=True)
                if kind == "vb":
                    pe.wait_ge(bdvs_ready, B)
                    last = pe.matmul(w[:], ONES[:], BDVS[:].rearrange("p b d -> p (b d)"), start=True, stop=True)
                if kind == "lx":
                    wait_used(pe, ("x2", n))
                    wait_used(pe, ("cm", 0))
                    for i in range(TB):
                        t = TB * n + i
                        last = pe.matmul(w[:, i * E1:(i + 1) * E1], XNT[:, t * P:(t + 1) * P], BDR[:, P:],
                                         start=(i == 0), stop=True, skip_group_check=True)
                if kind in RING_KINDS and kind != "o":
                    made(last, item)

            def turn_x(s, u):
                at_least(pe, xs_loaded[u % U], loaded(s, u))
                at_least(pe, xt_copied, s - 1)
                pe.transpose(WB[u % 2][:, 0:P], XSL[u % U][:, 0:D], IDF[:]).then_inc(x_turned, 1)

            def pe_step(st, u):
                if inside(st):
                    e = pe.value_load(SEXP[0:1, bass.ds(st, 1)], min_val=0, max_val=E1 - 1)
                    at_least(pe, xt_copied, st + 1)
                    at_least(pe, biased, st - 1)
                    pe.matmul(SC[:, u % 2, :], XTS[u % 2], W1[:, bass.ds(e * F1, F1)], start=True,
                              stop=True).then_inc(up_done, 1)
                if inside(st + 1):
                    turn_x(st + 1, u + 1)
                if inside(st - 1):
                    v = (u + 1) % 2
                    at_least(pe, gelu_done, st)
                    at_least(pe, gt_copied, st - 2)
                    for k in range(NF):
                        last = pe.transpose(SC[:, 2 + v, k * P:(k + 1) * P], GE[v][:, k * P:(k + 1) * P], IDF[:])
                    last.then_inc(g_turned, 1)
                if inside(st - 2):
                    e = pe.value_load(SEXP[0:1, bass.ds(st - 2, 1)], min_val=0, max_val=E1 - 1)
                    at_least(pe, gt_copied, st - 1)
                    at_least(pe, y_ready, st - 3)
                    for k in range(NF):
                        last = pe.matmul(DOWN[u % 2], GT[u % 2][:, k * P:(k + 1) * P],
                                         W2[:, bass.ds(e * (NF * D) + k * D, D)], start=(k == 0), stop=(k == NF - 1))
                    last.then_inc(down_done, 1)

            pe.wait_ge(slots_ready, 2)
            pe.wait_ge(w12_loaded, 32)
            wait_used(pe, ("vb", 0))
            turn_x(0, 0)
            run_slots(pe, pe_step, NS + 2)

        @block.vector
        def _(dve):
            n_seq = 0

            def seq(ins):
                nonlocal n_seq
                n_seq += 1
                ins.then_inc(dve_seq, 1)
                dve.wait_ge(dve_seq, n_seq)

            def variances(b):
                tiles = range(b * TB, (b + 1) * TB)
                for t in tiles:
                    last = dve.bn_aggr(MV[:, t], STATS[:, t])
                seq(last)
                r = slice(b * TB, (b + 1) * TB)
                dve.tensor_scalar(VE[:, r], MV[:, r, 1], LN_EPS, None, ALU.add).then_inc(var_ready, 1)

            def normalise(b, layer=0):
                dve.wait_ge(rstd_ready, layer * B + b + 1)
                for t in range(b * TB, (b + 1) * TB):
                    last = dve.tensor_scalar(XN[:, t, 0:D], X[:, t], MV[:, t, 0:1], RSTD[:, t:t + 1], ALU.subtract, ALU.mult)
                last.then_inc(xn_ready, 1)

            def rank_of(v, n):
                shape = [P, NT, n, n]
                mine = v.rearrange("p t (e o) -> p t e o", o=1).to_broadcast(shape)
                other = v.rearrange("p t (o e) -> p t o e", o=1).to_broadcast(shape)
                cmp = CMP[:, 0:NT * n * n].rearrange("p (t a c) -> p t a c", t=NT, a=n)
                eq = EQ[:, 0:NT * n * n].rearrange("p (t a c) -> p t a c", t=NT, a=n)
                low = LOW[:, 0:n, 0:n].rearrange("p (o a) c -> p o a c", o=1).to_broadcast(shape)
                dve.tensor_tensor(cmp, other, mine, ALU.is_gt)
                seq(dve.tensor_tensor(eq, other, mine, ALU.is_equal))
                seq(dve.tensor_tensor(eq, eq, low, ALU.mult))
                seq(dve.tensor_tensor(cmp, cmp, eq, ALU.add))
                seq(dve.tensor_reduce(RANK[:, :, 0:n], cmp, AX.X, ALU.add))

            def route():
                wait_used(dve, ("lg", 0))
                dve.wait_ge(const_ready, 2)
                bias = GB[:].rearrange("p (o e) -> p o e", o=1).to_broadcast([P, NT, E])
                seq(dve.tensor_tensor(SFC[:], SFC[:], bias, ALU.add))
                seq(dve.tensor_tensor(GS[:], SFC[:, :, 0:E:2], SFC[:, :, 1:E:2], ALU.add))
                rank_of(GS[:], 4)
                seq(dve.tensor_scalar(GS[:], RANK[:, :, 0:4], 2.0, None, ALU.is_lt))
                seq(dve.tensor_tensor(MASKED[:].rearrange("p t (g k) -> p t g k", k=2),
                                      SFC[:].rearrange("p t (g k) -> p t g k", k=2),
                                      GS[:].rearrange("p t (g o) -> p t g o", o=1).to_broadcast([P, NT, 4, 2]),
                                      ALU.mult))
                rank_of(MASKED[:], E)
                seq(dve.scalar_tensor_tensor(out=SFC[:], in0=RANK[:], scalar=2.0, in1=SFC[:],
                                             op0=ALU.is_lt, op1=ALU.mult))
                seq(dve.tensor_reduce(WSUM[:], SFC[:], AX.X, ALU.add))
                seq(dve.tensor_scalar(WSUM[:], WSUM[:], 1e-20, None, ALU.add))
                seq(dve.reciprocal(WSUM[:], WSUM[:]))
                seq(dve.tensor_scalar(WSUM[:], WSUM[:], 2.5, None, ALU.mult))
                seq(dve.tensor_tensor(SFC[:], SFC[:], WSUM[:].rearrange("p (t o) -> p t o", o=1)
                                      .to_broadcast([P, NT, E]), ALU.mult))
                seq(dve.tensor_copy(WPART[:, :, 0], SFC[:]))
                seq(dve.tensor_tensor(SFC[:], SFC[:], WPART[:, :, 0], ALU.subtract))
                seq(dve.tensor_copy(WPART[:, :, 1], SFC[:]))
                dve.tensor_tensor(WPART[:, :, 2], SFC[:], WPART[:, :, 1], ALU.subtract).then_inc(routed, 1)

            def choose(r):
                lo, hi = ROUTES[r]
                wide = [P, hi - lo, E1]
                col = lambda a: a.rearrange("p (t o) -> p t o", o=1).to_broadcast(wide)
                lg, oh, ex = LG[:, lo:hi], OH[:, lo:hi], EXC[:, lo:hi]
                seq(dve.tensor_reduce(MX[:, lo:hi], lg, AX.X, ALU.max))
                dve.tensor_tensor(ex, lg, col(MX[:, lo:hi]), ALU.subtract).then_inc(logits_centred, 1)
                seq(dve.tensor_tensor(oh, lg, col(MX[:, lo:hi]), ALU.is_equal))
                seq(dve.tensor_tensor(oh, oh, PRI[:].rearrange("p (o e) -> p o e", o=1).to_broadcast(wide), ALU.mult))
                seq(dve.tensor_reduce(MX[:, lo:hi], oh, AX.X, ALU.max))
                seq(dve.tensor_tensor(oh, oh, col(MX[:, lo:hi]), ALU.is_equal))
                for e in range(E1):
                    before = PFX[:, lo - 1, e:e + 1] if lo else 0.0
                    last = dve.tensor_tensor_scan(PFX[:, lo:hi, e], ONES[:, 0:hi - lo], oh[:, :, e], before,
                                                  ALU.mult, ALU.add)
                seq(last)
                dve.tensor_tensor(RUN[:, lo:hi], PFX[:, lo:hi], oh, ALU.subtract).then_inc(choice_ready, 1)
                dve.wait_ge(logits_exped, r + 1)
                seq(dve.tensor_reduce(MX[:, lo:hi], ex, AX.X, ALU.add))
                seq(dve.reciprocal(XN[:, lo:hi, COL_SCORE], MX[:, lo:hi]))

            def positions(r):
                lo, hi = ROUTES[r]
                w = bank(("rk", r))
                wait_made(dve, ("rk", r))
                q = EXC[:, lo:hi]
                ranks = w[:, 0:(hi - lo) * E1].rearrange("p (t e) -> p t e", e=E1)
                seq(dve.tensor_tensor(q, ranks, EBASE[:].rearrange("p (o e) -> p o e", o=1)
                                      .to_broadcast([P, hi - lo, E1]), ALU.add))
                seq(dve.tensor_tensor(q, q, OH[:, lo:hi], ALU.mult))
                seq(dve.tensor_reduce(MX[:, lo:hi], q, AX.X, ALU.add))
                dve.tensor_copy(POS[:, lo:hi], MX[:, lo:hi]).then_inc(pos_ready, 1)

            def slot_table():
                w = bank(("rk", 1))
                seq(dve.tensor_scalar(CNTI[:], w[0:1, 128:128 + E1], float(P - 1), None, ALU.add))
                seq(dve.tensor_scalar(CNTI[:], CNTI[:], P.bit_length() - 1, None, ALU.arith_shift_right))
                seq(dve.tensor_copy(CNTF[:], CNTI[:]))
                seq(dve.tensor_tensor_scan(INCL[:], ONES[0:1, 0:E1], CNTF[:], 0.0, ALU.mult, ALU.add))
                wide = [1, NS, E1]
                le = EQ[0:1, 0:NS * E1].rearrange("p (s e) -> p s e", e=E1)
                tl = CMP[0:1, 0:NS * E1].rearrange("p (s e) -> p s e", e=E1)
                seq(dve.tensor_tensor(le, INCL[:].rearrange("p (o e) -> p o e", o=1).to_broadcast(wide),
                                      SLOTI[:].rearrange("p (s o) -> p s o", o=1).to_broadcast(wide), ALU.is_le))
                dve.tensor_tensor(tl, le, CNTF[:].rearrange("p (o e) -> p o e", o=1).to_broadcast(wide), ALU.mult)
                seq(dve.tensor_reduce(STAB[:, 0], le, AX.X, ALU.add))
                seq(dve.tensor_reduce(STAB[:, 1], tl, AX.X, ALU.add))
                seq(dve.tensor_tensor(STAB[:, 2], SLOTI[:], STAB[:, 1], ALU.subtract))
                seq(dve.tensor_scalar(STAB[:, 2], STAB[:, 2], float(P), None, ALU.mult))
                dve.tensor_scalar(SEXP[:], STAB[:, 0], float(E1 - 1), None, ALU.min).then_inc(slots_ready, 1)
                dve.scalar_tensor_tensor(out=SBASE[:], in0=STAB[:, 0], scalar=float(CAP), in1=STAB[:, 2],
                                         op0=ALU.mult, op1=ALU.add).then_inc(slots_ready, 1)

            def head_attention():
                d = DS[:].rearrange("p (b i) h -> p b (i h)", b=B)
                seq(dve.tensor_reduce(SMX[:], d.rearrange("p b x -> p x b"), AX.X, ALU.max))
                wide = [P, B, TB * H]
                m = SMX[:].rearrange("p (o x) -> p o x", o=1).to_broadcast(wide)
                dve.tensor_tensor(d, d, m, ALU.subtract).then_inc(diag_centred, 1)
                dve.wait_ge(diag_exped, 1)
                seq(dve.tensor_reduce(SMX[:], d.rearrange("p b x -> p x b"), AX.X, ALU.add))
                seq(dve.reciprocal(SMX[:], SMX[:]))
                seq(dve.tensor_tensor(d, d, m, ALU.mult))

            def add_head_attention():
                wait_used(dve, ("vb", 0))
                for b in range(B):
                    shape = [P, TB, H, HD]
                    probs = DS[:, b * TB:(b + 1) * TB].rearrange("p i (h o) -> p i h o", o=1).to_broadcast(shape)
                    val = VBC[:, b].rearrange("p (o h e) -> p o h e", o=1, h=H).to_broadcast(shape)
                    seq(dve.tensor_tensor(ATT[:].rearrange("p (i h e) -> p i h e", i=TB, h=H), probs, val, ALU.mult))
                    x = X[:, b * TB:(b + 1) * TB].rearrange("p i d -> p (i d)")
                    seq(dve.tensor_tensor(x, x, ATT[:], ALU.add))

            for kind, n in plan:
                item = (kind, n)
                if kind == "ls":
                    dve.wait_ge(x_loaded[n], 16)
                    for t in range(n * TB, (n + 1) * TB):
                        last = dve.bn_stats(STATS[:, t], X[:, t])
                    seq(last)
                    variances(n)
                if kind == "ln":
                    normalise(n)
                    if n == 0:
                        dve.memset(YT[:], 0.0).then_inc(yt_cleared, 1)
                    if n == 1:
                        dve.wait_ge(small_w_loaded, 16 * 5)
                        seq(dve.tensor_tensor(WGSQ[:], WGN[:], WGN[:], ALU.mult))
                        dve.tensor_reduce(WGNORM[:], WGSQ[:], AX.X, ALU.add).then_inc(sumsq_ready, 1)
                if kind == "cw":
                    wait_made(dve, item)
                    w = bank(item)
                    dve.tensor_copy(WGNT[:], w[0:GATE, 3 * HD:3 * HD + E1])
                    seq(dve.tensor_copy(REP3[:], w[:, 0:3 * HD]))
                    for k, bd in enumerate((BDQ, BDK, BDV)):
                        rep = REP3[:, k * HD:(k + 1) * HD].rearrange("p (o e) -> p o e", o=1).to_broadcast([P, H, HD])
                        ins = dve.tensor_tensor(bd[:].rearrange("p (h e) -> p h e", h=H),
                                                BDMASK[:].rearrange("p (h e) -> p h e", h=H), rep, ALU.mult)
                    used(ins, item)
                if kind == "cm":
                    wait_made(dve, item)
                    used(dve.tensor_copy(BDR[:], bank(item)[:, 0:P + E1]), item)
                if kind == "l2":
                    normalise(n, 1)
                if kind == "lx":
                    wait_made(dve, item)
                    v = bank(item)[:, 0:TB * E1].rearrange("p (t e) -> p t e", t=TB)
                    used(dve.tensor_copy(LG[:, TB * n:TB * (n + 1)], v), item)
                    wait_used(dve, item)
                if kind == "d":
                    wait_made(dve, item)
                    t = slice(TB * n, TB * (n + 1))
                    v = bank(item)[:].rearrange("p (t d) -> p t d", t=TB)
                    pr = REST[:].rearrange("p (t d) -> p t d", t=TB)
                    used(dve.tensor_tensor(pr, v, XN[:, t, 0:D], ALU.mult), item)
                    wait_used(dve, item)
                    dve.tensor_scalar(BDVS[:, n], BDV[:], XS[:, n:n + 1], None, ALU.mult).then_inc(bdvs_ready, 1)
                    seq(dve.tensor_reduce(DS[:, t], pr.rearrange("p t (h e) -> p t h e", h=H), AX.X, ALU.add))
                if kind == "ra":
                    choose(n)
                if kind == "rk":
                    positions(n)
                    if n == 1:
                        slot_table()
                    used(dve.tensor_copy(JUNK[:], MX[:, 0:1]), item)
                if kind in "qk":
                    s = blk_of(kind, n)[3]
                    dve.wait_ge(first_part, s + 1)
                    part = PARTS[:, s % 3]
                    ins = dve.tensor_tensor(REST[:], bank(item)[:], part[:, 0], ALU.subtract)
                    used(ins, item)
                    wait_used(dve, item)
                    seq(dve.tensor_copy(part[:, 1], REST[:]))
                    dve.tensor_tensor(part[:, 2], REST[:], part[:, 1], ALU.subtract).then_inc(parts_ready, 1)
                    dve.wait_ge(parts_ready, s + 1)
                if kind == "rt":
                    dve.wait_ge(norm_ready, 1)
                    seq(dve.tensor_scalar(WGNORM[:], WGNORM[:], 1e-4, None, ALU.max))
                    seq(dve.reciprocal(WGNORM[:], WGNORM[:]))
                    dve.tensor_scalar(WGN[:], WGN[:], WGNORM[:, 0:1], None, ALU.mult).then_inc(wgn_ready, 1)
                    route()
                if kind == "g":
                    dve.wait_ge(sig_ready, n + 1)
                    used(dve.tensor_tensor(G[:, n % 2], SG[:, n % 2], bank(item)[:], ALU.mult), item)
                if kind == "u":
                    b, j = divmod(n, NJ)
                    wait_made(dve, item)
                    wait_used(dve, ("g", n))
                    if b >= 2 and j == 0:
                        wait_made(dve, ("o", TB * (b - 2) + TB - 1))
                    used(dve.tensor_tensor(HT[:, b % 2, j], G[:, n % 2], bank(item)[:], ALU.mult), item)
                if kind == "wt":
                    wait_made(dve, item)
                    if n >= 1:
                        wait_made(dve, ("w", (NJ - 1) * n - 1))
                    used(dve.tensor_copy(WTS[:], bank(item)[0:3 * E, 0:L // 2].bitcast(BF16)), item)
                if kind == "w":
                    b, j = divmod(n, NJ - 1)
                    wait_made(dve, item)
                    wait_used(dve, ("u", NJ * b + j))
                    used(dve.tensor_tensor(HT[:, b % 2, j], HT[:, b % 2, j], bank(item)[:], ALU.mult), item)
                if kind == "av" and n % TB == TB - 1:
                    m = n // TB
                    b, hg = divmod(m, 4)
                    dve.wait_ge(av_done, n + 1)
                    if b >= 1 and hg == 0:
                        wait_made(dve, ("n", TB * b - 1))
                    dve.tensor_copy(YS[:, hg], YT[:]).then_inc(yt_saved, 1)
                if kind == "n":
                    wait_made(dve, item)
                    i = n % TB
                    if n >= TB:
                        wait_used(dve, ("at", n - TB))
                    v = bank(item)[:, 0:144].rearrange("p (g c) -> p g c", g=4)
                    seq(dve.tensor_scalar(DEN[:].rearrange("p (g h) -> p g h", g=4), v[:, :, 32:36],
                                          2 * ATTN_EPS, CNT[:, i:i + 1], ALU.add, ALU.add))
                    seq(dve.reciprocal(RDEN[:], DEN[:]))
                    o = AO[:, i].rearrange("p (g h e) -> p g h e", g=4, h=4)
                    r = RDEN[:].rearrange("p (g h o) -> p g h o", g=4, o=1).to_broadcast([P, 4, 4, HD])
                    used(dve.tensor_tensor(o, v[:, :, 0:32].rearrange("p g (h e) -> p g h e", h=4), r, ALU.mult), item)
                if kind == "oa":
                    wait_made(dve, ("o", n))
                    used(dve.tensor_tensor(X[:, n], X[:, n], bank(("o", n))[:, 0:P], ALU.add), ("o", n))
                    wait_used(dve, ("o", n))
                    seq(dve.bn_stats(STATS[:, n], X[:, n]))
                    if n % TB == TB - 1:
                        variances(n // TB)

            head_attention()

            def dve_step(st, u):
                if inside(st):
                    e = dve.value_load(SEXP[0:1, bass.ds(st, 1)], min_val=0, max_val=E1 - 1)
                    at_least(dve, up_done, st + 1)
                    at_least(dve, gelu_done, st - 1)
                    dve.tensor_tensor(HB[u % 2], SC[:, u % 2, :], B1[:, bass.ds(e * F1, F1)],
                                      ALU.add).then_inc(biased, 1)
                if inside(st - 2):
                    e = dve.value_load(SEXP[0:1, bass.ds(st - 2, 1)], min_val=0, max_val=E1 - 1)
                    at_least(dve, down_done, st - 1)
                    at_least(dve, y_scattered[u % 2], 8 * st - (8 * (u % 2) + 16))
                    ins = dve.tensor_tensor(YO[u % 2], DOWN[u % 2], B2[:, bass.ds(e * D, D)], ALU.add)
                    ins.then_inc(y_summed, 1)
                    dve.wait_ge(y_summed, st - 1)
                    dve.tensor_scalar(YO[u % 2], YO[u % 2], SCORE[(u - 2) % U][:], None,
                                      ALU.mult).then_inc(y_ready, 1)
                if inside(st):
                    at_least(dve, xs_loaded[u], loaded(st, u))
                    dve.tensor_copy(SCORE[u][:], XSL[u][:, COL_SCORE:COL_SCORE + 1])
                    dve.tensor_tensor(ROW[u][:], XSL[u][:, COL_ID:COL_ID + 1], PADROW[:, bass.ds(st, 1)],
                                      ALU.min).then_inc(ids_kept, 1)

            dve.wait_ge(b12_loaded, 32)
            run_slots(dve, dve_step, NS + 2)
            add_head_attention()
            for b in range(B):
                dve.wait_ge(y_loaded[b], 16)
                x = X[:, b * TB:(b + 1) * TB]
                dve.tensor_tensor(x, x, YG[:, b * TB:(b + 1) * TB], ALU.add).then_inc(out_ready, 1)


_TURNED = {"L0_attn_Wq", "L0_attn_Wk", "L0_attn_Wv", "L0_attn_Wo", "L1_attn_Wv", "L1_ffn_w_red"}
_INS = ["L0_attn_hidden_states", "L0_attn_Wq", "L0_attn_Wk", "L0_attn_Wv", "L0_attn_Wo", "L0_ffn_gate_w",
        "L0_ffn_gate_bias", "L0_ffn_w_gate", "L0_ffn_w_up", "L0_ffn_w_down", "L0_ffn_sw_gate", "L0_ffn_sw_up",
        "L0_ffn_sw_down", "L1_attn_Wq", "L1_attn_Wk", "L1_attn_Wv", "L1_ffn_w_red", "L1_ffn_wg", "L1_ffn_w1",
        "L1_ffn_b1", "L1_ffn_w2", "L1_ffn_b2"]
_OUTS = [((B, L, D), "float32")]


def kernel(**inputs):
    import numpy as _np
    import concourse.bacc as _bacc
    from concourse import mybir as _mybir
    from concourse.bass_utils import run_bass_kernel_spmd as _run

    nc = _bacc.Bacc("TRN2", target_bir_lowering=False, num_devices=1)
    arrays, args = {}, []
    for name in _INS:
        a = _np.asarray(inputs[name])
        a = _np.ascontiguousarray(a.T if name in _TURNED else a)
        arrays[f"in_{name}_dram"] = a
        args.append(nc.dram_tensor(f"in_{name}_dram", a.shape, _mybir.dt.from_np(a.dtype), kind="ExternalInput").ap())
    for i, (shape, dtype) in enumerate(_OUTS):
        dt = _mybir.dt.from_np(_np.dtype(dtype))
        args.append(nc.dram_tensor(f"out_{i}_dram", shape, dt, kind="ExternalOutput").ap())
    two_layers(nc, *args)
    r = _run(nc, [arrays], core_ids=[0])
    got = tuple(r.results[0][f"out_{i}_dram"] for i in range(len(_OUTS)))
    return got[0]
```
